# Optimizing a Trainium2 kernel written in Bass

```python
import numpy as np
import jax
import jax.numpy as jnp

def _softmax(x, axis=-1):
    return jax.nn.softmax(x, axis=axis)

def _gelu(x):
    return jax.nn.gelu(x, approximate=True)

def _silu(x):
    return jax.nn.silu(x)

def _sigmoid(x):
    return jax.nn.sigmoid(x)

def _layernorm(x, axis=-1, eps=1e-05):
    m = jnp.mean(x, axis=axis, keepdims=True)
    v = jnp.var(x, axis=axis, keepdims=True)
    return (x - m) / jnp.sqrt(v + eps)

def _scatter_add(tgt, idx, src, axis=0):
    return tgt.at[idx].add(src)

def _segment_sum(src, seg, n):
    return jax.ops.segment_sum(src, seg, n)
kernel_name = 'mk_sandwich_d1_jaxref_r8_87afa9'

def setup_inputs(seed: int=0):
    np.random.seed(seed)
    _w = jnp.asarray

    def _L0_attn_setup():
        import jax, jax.numpy as jnp
        import numpy as np
        from jax import lax
        D_MODEL = 128
        N_HEADS = 8
        D_HEAD = 64
        D_INNER = N_HEADS * D_HEAD
        B, T = (4, 512)
        LN_EPS = 1e-05
        NORM_EPS = 1e-12
        key = jax.random.key(seed)
        ks = jax.random.split(key, 6)
        s_proj = (2.0 / (D_MODEL + D_INNER)) ** 0.5
        x = jax.random.normal(ks[0], (B, T, D_MODEL), jnp.float32)
        Wq = jax.random.normal(ks[1], (D_MODEL, D_INNER), jnp.float32) * s_proj
        Wk = jax.random.normal(ks[2], (D_MODEL, D_INNER), jnp.float32) * s_proj
        Wv = jax.random.normal(ks[3], (D_MODEL, D_INNER), jnp.float32) * s_proj
        Wa = jax.random.normal(ks[4], (D_MODEL, D_INNER), jnp.float32) * s_proj
        ba = jnp.full((D_INNER,), 3.0, jnp.float32)
        Wo = jax.random.normal(ks[5], (D_INNER, D_MODEL), jnp.float32) * s_proj
        gamma = jnp.ones((D_MODEL,), jnp.float32)
        beta = jnp.zeros((D_MODEL,), jnp.float32)
        return {'x': x, 'Wq': Wq, 'Wk': Wk, 'Wv': Wv, 'Wa': Wa, 'ba': ba, 'Wo': Wo, 'gamma': gamma, 'beta': beta}
    _L0_attn_in = _L0_attn_setup()

    def _L0_ffn_setup():
        import jax, jax.numpy as jnp
        import numpy as np
        B, S, D = (1, 256, 128)
        E, K, F = (8, 2, 176)
        NS = 2
        SCALE = 2.5

        def _swiglu_mlp(x, wg, wu, wd):
            return jax.nn.silu(x @ wg) * (x @ wu) @ wd
        key = jax.random.key(seed)
        ks = jax.random.split(key, 8)
        s = 0.02
        return {'hidden_states': jax.random.normal(ks[0], (B, S, D), jnp.float32), 'gate_w': jax.random.normal(ks[1], (E, D), jnp.float32) * s, 'w_gate': jax.random.normal(ks[2], (E, D, F), jnp.float32) * s, 'w_up': jax.random.normal(ks[3], (E, D, F), jnp.float32) * s, 'w_down': jax.random.normal(ks[4], (E, F, D), jnp.float32) * s, 'sw_gate': jax.random.normal(ks[5], (D, F * NS), jnp.float32) * s, 'sw_up': jax.random.normal(ks[6], (D, F * NS), jnp.float32) * s, 'sw_down': jax.random.normal(ks[7], (F * NS, D), jnp.float32) * s}
    _L0_ffn_in = _L0_ffn_setup()
    _d = {'L0_attn_x': _L0_attn_in['x'], 'L0_attn_Wq': _L0_attn_in['Wq'], 'L0_attn_Wk': _L0_attn_in['Wk'], 'L0_attn_Wv': _L0_attn_in['Wv'], 'L0_attn_Wa': _L0_attn_in['Wa'], 'L0_attn_ba': _L0_attn_in['ba'], 'L0_attn_Wo': _L0_attn_in['Wo'], 'L0_attn_gamma': _L0_attn_in['gamma'], 'L0_attn_beta': _L0_attn_in['beta'], 'L0_ffn_gate_w': _L0_ffn_in['gate_w'], 'L0_ffn_w_gate': _L0_ffn_in['w_gate'], 'L0_ffn_w_up': _L0_ffn_in['w_up'], 'L0_ffn_w_down': _L0_ffn_in['w_down'], 'L0_ffn_sw_gate': _L0_ffn_in['sw_gate'], 'L0_ffn_sw_up': _L0_ffn_in['sw_up'], 'L0_ffn_sw_down': _L0_ffn_in['sw_down']}
    _x0 = _d['L0_attn_x']
    _d['L0_attn_x'] = jax.random.normal(jax.random.fold_in(jax.random.key(seed), 1), (8, 1024, 128), dtype=_x0.dtype)
    del _x0
    return _d

def reference(L0_attn_x, L0_attn_Wq, L0_attn_Wk, L0_attn_Wv, L0_attn_Wa, L0_attn_ba, L0_attn_Wo, L0_attn_gamma, L0_attn_beta, L0_ffn_gate_w, L0_ffn_w_gate, L0_ffn_w_up, L0_ffn_w_down, L0_ffn_sw_gate, L0_ffn_sw_up, L0_ffn_sw_down):

    def _L0_attn_ref(x, Wq, Wk, Wv, Wa, ba, Wo, gamma, beta):
        import jax, jax.numpy as jnp
        import numpy as np
        from jax import lax
        D_MODEL = 128
        N_HEADS = 8
        D_HEAD = 64
        D_INNER = N_HEADS * D_HEAD
        B, T = (4, 512)
        LN_EPS = 1e-05
        NORM_EPS = 1e-12
        Bx, Tx, _ = x.shape
        residual = x
        mu = jnp.mean(x, axis=-1, keepdims=True)
        var = jnp.var(x, axis=-1, keepdims=True)
        xn = (x - mu) / jnp.sqrt(var + LN_EPS) * gamma + beta

        def heads(y):
            return jnp.moveaxis(y.reshape(Bx, Tx, N_HEADS, D_HEAD), 1, 0)
        q = heads(xn @ Wq)
        k = heads(xn @ Wk)
        v = heads(xn @ Wv)
        alpha = jax.nn.sigmoid(heads(xn @ Wa + ba))
        knorm = jnp.linalg.norm(k, axis=-1, keepdims=True)
        k = k / jnp.maximum(knorm, NORM_EPS)

        def step(S, inp):
            q_t, k_t, v_t, a_t = inp
            S = a_t[..., None] * S + k_t[..., None] * v_t[..., None, :]
            o_t = jnp.einsum('bhji,bhj->bhi', S, q_t)
            return (S, o_t)
        S0 = jnp.zeros((Bx, N_HEADS, D_HEAD, D_HEAD), x.dtype)
        _, outs = lax.scan(step, S0, (q, k, v, alpha))
        out = jnp.moveaxis(outs, 0, 1).reshape(Bx, Tx, D_INNER) @ Wo
        return out + residual

    def _L0_ffn_ref(hidden_states, gate_w, w_gate, w_up, w_down, sw_gate, sw_up, sw_down):
        import jax, jax.numpy as jnp
        import numpy as np
        B, S, D = (1, 256, 128)
        E, K, F = (8, 2, 176)
        NS = 2
        SCALE = 2.5

        def _swiglu_mlp(x, wg, wu, wd):
            return jax.nn.silu(x @ wg) * (x @ wu) @ wd
        identity = hidden_states
        x = hidden_states.reshape(-1, hidden_states.shape[-1])
        T = x.shape[0]
        logits = x.astype(jnp.float32) @ gate_w.astype(jnp.float32).T
        scores = jax.nn.softmax(logits, axis=-1)
        topk_w, topk_i = jax.lax.top_k(scores, K)
        topk_w = topk_w / (topk_w.sum(-1, keepdims=True) + 1e-20) * SCALE
        combine = jnp.zeros((T, E), jnp.float32).at[jnp.arange(T)[:, None], topk_i].set(topk_w)
        g = jax.nn.silu(jnp.einsum('td,edf->etf', x, w_gate)) * jnp.einsum('td,edf->etf', x, w_up)
        expert_out = jnp.einsum('etf,efd->etd', g, w_down)
        y = jnp.einsum('te,etd->td', combine, expert_out).astype(x.dtype)
        y = y.reshape(identity.shape)
        return y + _swiglu_mlp(identity, sw_gate, sw_up, sw_down)
    x = L0_attn_x
    x = x + _layernorm(_L0_attn_ref(_layernorm(x, axis=-1), L0_attn_Wq, L0_attn_Wk, L0_attn_Wv, L0_attn_Wa, L0_attn_ba, L0_attn_Wo, L0_attn_gamma, L0_attn_beta), axis=-1)
    x = x + _layernorm(_L0_ffn_ref(_layernorm(x, axis=-1), L0_ffn_gate_w, L0_ffn_w_gate, L0_ffn_w_up, L0_ffn_w_down, L0_ffn_sw_gate, L0_ffn_sw_up, L0_ffn_sw_down), axis=-1)
    return x

_drawn_inputs = setup_inputs


def setup_inputs(seed=0):
    import zlib

    import numpy as np

    out = dict(_drawn_inputs(seed))
    spreads = {'L0_attn_ba': (3.0, 0.2), 'L0_attn_gamma': (1.0, 0.2), 'L0_attn_beta': (0.0, 0.1)}
    factors = {}
    for name, (base, spread) in spreads.items():
        noise = np.random.default_rng([zlib.crc32(name.encode()), seed]).standard_normal(out[name].shape)
        drawn = base * np.exp(spread * noise) if base else spread * noise
        out[name] = jnp.asarray(drawn.astype(out[name].dtype))
    for name, factor in factors.items():
        out[name] = (out[name] * factor).astype(out[name].dtype)
    return out
```

```python
import concourse.bass as bass
from concourse import mybir
from contextlib import ExitStack

F32 = mybir.dt.float32
F32R = mybir.dt.float32r
U32 = mybir.dt.uint32
ALU = mybir.AluOpType
ACT = mybir.ActivationFunctionType
AX = mybir.AxisListType

B, SEQ, D = 8, 1024, 128
H, DH = 8, 64
P = 128
NT = 4
GT = NT * P
NG = B * SEQ // GT
NP_ = H // 2
SEQ_GROUPS = SEQ // GT
E, F, NS, TOPK, SCALE = 8, 176, 2, 2, 2.5
EF = E * F
FT = EF // P
SF = F * NS
FTILES = [(t, P) for t in range(FT)] + [(FT, P), (FT + 1, P), (FT + 2, SF - 2 * P)]
NF = len(FTILES)
LN_EPS, NORM_EPS = 1e-5, 1e-12
LEVELS = [0, 1, 2, 4, 8, 16, 32, 64]
BLOCKS = LEVELS.index(16)
BANK = {l: 1 - l % 2 for l in range(1, len(LEVELS))}
T_AT = {2: 0, 4: 256, 8: 384, 16: 448, 32: 480, 64: 496, 128: 504}


class AttentionSems:

    def __init__(self, sem):
        self.link = sem("link")
        self.var_ready = sem("var_ready")
        self.rstd_ready = sem("rstd_ready")
        self.wo_done = sem("wo_done")
        self.wo_read = sem("wo_read")
        self.proj_done = sem("proj_done")
        self.act_evac = sem("act_evac")
        self.sq_read = sem("sq_read")
        self.n2_ready = sem("n2_ready")
        self.rn_ready = sem("rn_ready")
        self.v_scaled = sem("v_scaled")
        self.q_one = sem("q_one")
        self.t_ready = sem("t_ready")
        self.xhat_ready = sem("xhat_ready")
        self.xt_done = sem("xt_done")
        self.xn_tmp = sem("xn_tmp")
        self.xh_ready = sem("xh_ready")
        self.lv_done = sem("lv_done")
        self.merged = sem("merged")
        self.placed = sem("placed")
        self.q_up = sem("q_up")
        self.k_up = sem("k_up")
        self.carried = sem("carried")
        self.kv_done = sem("kv_done")
        self.s_step = sem("s_step")
        self.within_done = sem("within_done")
        self.o_done = sem("o_done")
        self.ot_ready = sem("ot_ready")
        self.xh2_ready = sem("xh2_ready")
        self.xt2_ready = sem("xt2_ready")
        self.all = [self.link, self.var_ready, self.rstd_ready, self.wo_done, self.wo_read, self.proj_done, self.act_evac,
                    self.sq_read, self.n2_ready, self.rn_ready, self.v_scaled, self.q_one, self.t_ready, self.xhat_ready,
                    self.xt_done, self.xn_tmp, self.xh_ready, self.lv_done, self.merged, self.placed, self.q_up, self.k_up,
                    self.carried, self.kv_done, self.s_step, self.within_done, self.o_done, self.ot_ready,
                    self.xh2_ready, self.xt2_ready]


class MoeSems:

    def __init__(self, sem):
        self.link = sem("link")
        self.var_ready = sem("var_ready")
        self.rstd_ready = sem("rstd_ready")
        self.exp_in = sem("exp_in")
        self.exp_done = sem("exp_done")
        self.wh_ready = sem("wh_ready")
        self.routed = sem("routed")
        self.xhat_ready = sem("xhat_ready")
        self.xt_done = sem("xt_done")
        self.ct_done = sem("ct_done")
        self.xtmp = sem("xtmp")
        self.xh_ready = sem("xh_ready")
        self.g_done = sem("g_done")
        self.silu_done = sem("silu_done")
        self.u_done = sem("u_done")
        self.tu_done = sem("tu_done")
        self.hg_done = sem("hg_done")
        self.down_done = sem("down_done")
        self.x_final = sem("x_final")
        self.all = [self.link, self.var_ready, self.rstd_ready, self.exp_in, self.exp_done, self.wh_ready, self.routed,
                    self.xhat_ready, self.xt_done, self.ct_done, self.xtmp, self.xh_ready, self.g_done, self.silu_done,
                    self.u_done, self.tu_done, self.hg_done, self.down_done, self.x_final]


class Link:

    def __init__(self, engine, sem):
        self.engine, self.sem, self.n = engine, sem, 0

    def __call__(self, instruction):
        self.n += 1
        instruction.then_inc(self.sem, 1)
        self.engine.wait_ge(self.sem, self.n)


class Norms:

    def __init__(self, nc, s, st, mv, ve, rs, half):
        self.nc, self.s, self.st, self.mv, self.ve, self.rs, self.half = nc, s, st, mv, ve, rs, half
        self.n = 0

    def roots(self, pool, n):
        pool.wait_ge(self.s.var_ready, n)
        self.nc.gpsimd.tensor_tensor(self.rs[:, :], self.ve[:, :], self.half[:, 0:NT], ALU.pow).then_inc(self.s.rstd_ready, 1)

    def __call__(self, v, link, src, dst):
        self.n += 1
        nc, s = self.nc, self.s
        for t in range(NT):
            last = nc.vector.bn_stats(self.st[:, t, :], src(t))
        link(last)
        for t in range(NT):
            last = nc.vector.bn_aggr(self.mv[:, t, :], self.st[:, t, :])
        link(last)
        nc.vector.tensor_scalar(self.ve[:, :], self.mv[:, :, 1], LN_EPS, None, ALU.add).then_inc(s.var_ready, 1)
        v.wait_ge(s.rstd_ready, self.n)
        for t in range(NT):
            last = self.nc.vector.tensor_scalar(dst(t), src(t), self.mv[:, t, 0:1], self.rs[:, t:t + 1], ALU.subtract, ALU.mult)
        return last


def build(nc, x, Wq, Wk, Wv, Wa, ba, Wo, gamma, beta, gate_w, w_gate, w_up, w_down, sw_gate, sw_up, sw_down,
          c_ident, c_masks, c_sel, c_rank, y):
    x_g = x.rearrange("b (u t p) d -> p (b u) t d", t=NT, p=P)
    y_g = y.rearrange("b (u t p) d -> p (b u) t d", t=NT, p=P)
    top = ExitStack()
    with top:
        def sbuf(ctx, name, shape, dt=F32):
            return ctx.enter_context(nc.sbuf_tensor(name, shape, dt))

        def sem(name):
            return top.enter_context(nc.semaphore(name))

        def clear(engine, used):
            for s in used.all:
                engine.sem_clear(s)

        X = sbuf(top, "X", [P, NG * NT, D])
        LG = sbuf(top, "LG", [P, NG * NT, E])
        ident = sbuf(top, "ident", [P, P])
        ST = sbuf(top, "ST", [P, NT, 6])
        MV = sbuf(top, "MV", [P, NT, 2])
        VE = sbuf(top, "VE", [P, NT])
        RS = sbuf(top, "RS", [P, NT])
        HALF = sbuf(top, "HALF", [P, NT * H])
        XHAT = sbuf(top, "XHAT", [P, NT, D])
        XH2 = sbuf(top, "XH2", [P, NT, D])
        OSUM = sbuf(top, "OSUM", [P, NT, D])
        XTMP = sbuf(top, "XTMP", [P, GT])
        XH = sbuf(top, "XH", [P, 2, GT], F32R)
        XL = sbuf(top, "XL", [P, 2, GT], F32R)

        load_first, load_rest, load_ffn, stored = sem("load_first"), sem("load_rest"), sem("load_ffn"), sem("stored")
        load_w, load_c = sem("load_w"), sem("load_c")

        def norms(s):
            return Norms(nc, s, ST, MV, VE, RS, HALF)

        def split3(out, wh, wl, xh, xl):
            nc.tensor.matmul(out, wl, xh, start=True, stop=False)
            nc.tensor.matmul(out, wh, xl, start=False, stop=False)
            return nc.tensor.matmul(out, wh, xh, start=False, stop=True)

        att = ExitStack()
        with att:
            WH = sbuf(att, "WH", [P, 4, H * DH], F32R)
            WL = sbuf(att, "WL", [P, 4, H * DH], F32R)
            WO = sbuf(att, "WO", [P, NP_, D])
            GW = sbuf(att, "GW", [P, E])
            BA = sbuf(att, "BA", [P, NP_])
            GB = sbuf(att, "GB", [P, 2])
            MASK = sbuf(att, "MASK", [P, 4, P], U32)
            X1 = sbuf(att, "X1", [P, 2, NT, D])
            Q0 = sbuf(att, "Q0", [P, 2, 2, GT])
            Q = sbuf(att, "Q", [P, NP_, 2, GT])
            K = sbuf(att, "K", [P, NP_, GT])
            KSQ = sbuf(att, "KSQ", [P, 2, GT])
            N2 = sbuf(att, "N2", [P, NT, H])
            RN = sbuf(att, "RN", [P, NT, H])
            AL = sbuf(att, "AL", [P, NP_, GT])
            TT = sbuf(att, "TT", [P, NP_, GT])
            V = sbuf(att, "V", [P, NT, H * DH])
            AT = sbuf(att, "AT", [P, 2, NT * 2, P])
            OT = sbuf(att, "OT", [P, NP_, GT])
            KTOK = sbuf(att, "KTOK", [P, 2, NT, P])
            S = sbuf(att, "S", [P, NP_, NT + 1, P])
            XT2 = sbuf(att, "XT2", [P, GT])
            RAW = Q[:, :, 0, :]
            L = [att.enter_context(nc.psum_tensor(f"L{i}", [P, 2 * NT * P], F32)) for i in range(2)]
            PJ = [att.enter_context(nc.psum_tensor(f"PJ{i}", [P, GT], F32)) for i in range(2)]
            OB = [att.enter_context(nc.psum_tensor(f"OB{i}", [P, GT], F32)) for i in range(2)]

            def xt_stage_dve(v, s, done, got):
                v.wait_ge(s.xt_done, 1)
                nc.vector.tensor_scalar(XTMP[:, :], got, GB[:, 0:1], GB[:, 1:2], ALU.mult, ALU.add).then_inc(done, 1)

            def double_norm(v, link, norm, g, par, ready):
                link(norm(v, link, lambda t: group_tile(g, t), lambda t: X1[:, par, t, :]))
                norm(v, link, lambda t: X1[:, par, t, :], lambda t: XHAT[:, t, :]).then_inc(ready, 1)

            def group_tile(g, t):
                if isinstance(g, int):
                    return X[:, g * NT + t, :]
                return X[:, bass.ds(g * NT + t, 1), :].rearrange("p o d -> p (o d)")

            def group_of(tensor, g):
                return tensor[:, bass.ds(g * NT, NT), :] if not isinstance(g, int) else tensor[:, g * NT:(g + 1) * NT, :]

            A = [AttentionSems(lambda name: sem(f"a{i}_{name}")) for i in range(2)]

            with nc.Block() as block:
                s = A[1]

                @block.sync
                def _(sp):
                    sp.dma_start(X[:, 0:NT, :], x_g[:, 0, :, :]).then_inc(load_first, 16)
                    for i, w in enumerate((Wq, Wk, Wv, Wa)):
                        sp.dma_start(RAW[:, i, :], w).then_inc(load_w, 16)
                    sp.dma_start(ident[:, :], c_ident).then_inc(load_c, 16)
                    with nc.allow_non_contiguous_dma(reason="small vectors put on partitions"):
                        sp.dma_start(BA[:, :], ba.rearrange("(n p) -> p n", p=P)).then_inc(load_c, 16)
                        sp.dma_start(GB[:, 0:1], gamma.rearrange("(p o) -> p o", o=1)).then_inc(load_c, 16)
                        sp.dma_start(GB[:, 1:2], beta.rearrange("(p o) -> p o", o=1)).then_inc(load_c, 16)
                        sp.dma_start(GW[:, :], gate_w.rearrange("e d -> d e")).then_inc(load_c, 16)
                    sp.dma_start(MASK[:, :, :], c_masks).then_inc(load_c, 16)
                    sp.dma_start(WO[:, :, :], Wo.rearrange("(n p) d -> p n d", p=P)).then_inc(load_c, 16)
                    sp.dma_start(X[:, NT:, :].rearrange("p (g t) d -> p g t d", t=NT), x_g[:, 1:, :, :]).then_inc(load_rest, 16)
                    sp.wait_ge(load_c, 7 * 16)

                @block.gpsimd
                def _(pool):
                    nc.gpsimd.memset(HALF[:, :], -0.5).then_inc(s.q_one, 1)
                    nc.gpsimd.memset(Q0[:, :, :, :], 0.0)
                    pool.wait_ge(s.q_one, 1)
                    norm = norms(s)
                    norm.roots(pool, 1)
                    norm.roots(pool, 2)
                    pool.wait_ge(s.act_evac, 1)
                    nc.gpsimd.tensor_tensor(WL[:, :, :], RAW, WH[:, :, :].bitcast(F32), ALU.subtract).then_inc(s.q_up, 1)
                    pool.wait_ge(s.xh_ready, 1)
                    nc.gpsimd.tensor_tensor(XL[:, 0, :], XTMP[:, :], XH[:, 0, :].bitcast(F32), ALU.subtract)

                @block.scalar
                def _(act):
                    act.wait_ge(load_w, 4 * 16)
                    nc.scalar.activation(WH[:, :, :], RAW, ACT.Copy).then_inc(s.act_evac, 1)
                    act.wait_ge(s.xn_tmp, 1)
                    nc.scalar.activation(XH[:, 0, :], XTMP[:, :], ACT.Copy).then_inc(s.xh_ready, 1)

                @block.tensor
                def _(pe):
                    pe.wait_ge(load_c, 7 * 16)
                    pe.wait_ge(s.xhat_ready, 1)
                    for t in range(NT):
                        last = nc.tensor.transpose(OB[1][:, t * P:(t + 1) * P], XHAT[:, t, :], ident[:, :])
                    last.then_inc(s.xt_done, 1)

                @block.vector
                def _(v):
                    link, norm = Link(v, s.link), norms(s)
                    v.wait_ge(load_first, 16)
                    double_norm(v, link, norm, 0, 0, s.xhat_ready)
                    v.wait_ge(load_c, 7 * 16)
                    xt_stage_dve(v, s, s.xn_tmp, OB[1][:, :])

            START = [("n", t) for t in range(NT)] + [(w, p) for p in (0, 1) for w in "kqa"]
            TAIL = [("x", 0), ("k", 2), ("q", 2), ("a", 2)]
            MIDDLE = [("v", t) for t in range(NT)] + [("r", 0), ("r", 1)]
            BEFORE_SECOND = [(w, 3) for w in "kqa"] + [("l", 0)]
            END = [("r", 2), ("r", 3)]

            def attention_block(g, hf, first=False, final=False):
                s, other = A[hf], A[1 - hf]
                items = [it for it in START + TAIL + MIDDLE + BEFORE_SECOND + END if not (first and it[0] in "xl")]
                at_item = {it: i for i, it in enumerate(items)}
                taken = [sum(1 for w, _ in items[:i + 1] if (w == "v") == (items[i][0] == "v")) for i in range(len(items))]
                taken_sem = lambda i: s.v_scaled if items[i][0] == "v" else s.act_evac
                evac = lambda *item: taken[at_item[item]]
                NL = len(LEVELS)
                lv = lambda c, l, i: (c * NL + l) * 2 + i + 1
                up = lambda c, l, i: (c * (NL - 1) + l - 1) * 2 + i + 1
                mg = lambda c, l, i: (c * BLOCKS + l) * 2 + i + 1
                pl = lambda c, l, i: (c * (NL - BLOCKS) + l - BLOCKS) * 2 + i + 1

                with nc.Block() as block:
                    @block.sync
                    def _(sp):
                        clear(sp, other)

                    @block.tensor
                    def _(pe):
                        def item(kind, n):
                            if (kind, n) not in at_item:
                                return
                            i = at_item[kind, n]
                            bank = PJ[i % 2]
                            if i >= 2:
                                pe.wait_ge(taken_sem(i - 2), taken[i - 2])
                            if kind in "kqa":
                                w = "qkva".index(kind)
                                cols = slice(n * P, (n + 1) * P)
                                last = split3(bank[:, :], WH[:, w, cols], WL[:, w, cols], XH[:, hf, :], XL[:, hf, :])
                            elif kind in "nv":
                                w, toks = "qkva".index("k" if kind == "n" else "v"), slice(n * P, (n + 1) * P)
                                last = split3(bank[:, :], XH[:, hf, toks], XL[:, hf, toks], WH[:, w, :], WL[:, w, :])
                            elif kind == "x":
                                pe.wait_ge(s.xh2_ready, 1)
                                for t in range(NT):
                                    last = nc.tensor.transpose(bank[:, t * P:(t + 1) * P], XH2[:, t, :], ident[:, :])
                            elif kind == "l":
                                pe.wait_ge(s.act_evac, evac("x", 0))
                                for t in range(NT):
                                    last = nc.tensor.matmul(bank[:, t * E:(t + 1) * E], XT2[:, t * P:(t + 1) * P], GW[:, :],
                                                            start=True, stop=True)
                            else:
                                pe.wait_ge(s.k_up, up(n // 2, NL - 1, n % 2))
                                for t in range(NT):
                                    last = nc.tensor.transpose(bank[:, t * P:(t + 1) * P], K[:, n, t * P:(t + 1) * P], ident[:, :])
                            last.then_inc(s.proj_done, 1)

                        def level(c, l, i):
                            p, sz = 2 * c + i, LEVELS[l]
                            if l == 0:
                                pe.wait_ge(s.act_evac, evac("q", p))
                                if c:
                                    pe.wait_ge(s.s_step, NT * (i + 1))
                                    if i and not final:
                                        pe.wait_ge(s.xn_tmp, 1)
                            elif l == 1:
                                pe.wait_ge(s.q_one, p + 1)
                                pe.wait_ge(s.merged, mg(c, 0, i))
                            else:
                                pe.wait_ge(s.q_up, up(c, l - 1, i))
                                pe.wait_ge(s.k_up, up(c, l - 1, i))
                                if 2 < l < BLOCKS + 2:
                                    pe.wait_ge(s.merged, mg(c, l - 2, i))
                                elif l >= BLOCKS + 2:
                                    pe.wait_ge(s.placed, pl(c, l - 2, i))
                            for t in range(NT):
                                k = K[:, p, t * P:(t + 1) * P]
                                if l == 0:
                                    last = nc.tensor.matmul(L[i][:, t * 2 * P:(t + 1) * 2 * P], k, Q0[:, i, :, t * P:(t + 1) * P],
                                                            start=True, stop=True)
                                    continue
                                q = Q[:, p, :, t * P:(t + 1) * P]
                                at = BANK[l] * GT
                                if l < BLOCKS:
                                    last = nc.tensor.matmul(L[i][:, at + t * P:at + (t + 1) * P], k,
                                                            q.rearrange("p h (m two s) -> p h m two s", two=2, s=sz)[:, :, :, 1, :],
                                                            start=True, stop=True)
                                    continue
                                for b in range(0, P, 2 * sz):
                                    last = nc.tensor.matmul(L[i][b:b + sz, at + 2 * t * sz:at + 2 * (t + 1) * sz], k[:, b:b + sz],
                                                            q[:, :, b + sz:b + 2 * sz], start=True, stop=True)
                            last.then_inc(s.lv_done, 1)

                        def both(c, l):
                            level(c, l, 0)
                            level(c, l, 1)

                        def within_tiles(c, i):
                            p = 2 * c + i
                            pe.wait_ge(s.merged, mg(c, BLOCKS - 1, i))
                            pe.wait_ge(s.placed, pl(c, NL - 1, i))
                            pe.wait_ge(s.v_scaled, NT)
                            if c:
                                pe.wait_ge(s.ot_ready, i + 1)
                            elif i == 0 and not first:
                                pe.wait_ge(s.wo_read, 1)
                            for t in range(NT):
                                for h in range(2):
                                    last = nc.tensor.matmul(OB[i][h * DH:(h + 1) * DH, t * P:(t + 1) * P],
                                                            V[:, t, (2 * p + h) * DH:(2 * p + h + 1) * DH],
                                                            AT[:, i, 2 * t + h, :], start=(t == 0),
                                                            stop=(hf == 0 and t == 0), skip_group_check=True)
                            last.then_inc(s.within_done, 1)

                        def key_values(c, i):
                            p = 2 * c + i
                            pe.wait_ge(s.act_evac, evac("r", p))
                            for t in range(NT):
                                last = nc.tensor.matmul(L[i][:, t * P:(t + 1) * P], KTOK[:, i, t, :],
                                                        V[:, t, p * P:(p + 1) * P], start=True, stop=True)
                            last.then_inc(s.kv_done, 1)

                        def from_states(c, i):
                            p = 2 * c + i
                            pe.wait_ge(s.q_up, up(c, NL - 1, i))
                            for t in range(1 if hf == 0 else 0, NT):
                                if t:
                                    pe.wait_ge(s.s_step, p * NT + t)
                                else:
                                    pe.wait_ge(s.carried, 1)
                                for h in range(2):
                                    last = nc.tensor.matmul(OB[i][h * DH:(h + 1) * DH, t * P:(t + 1) * P],
                                                            S[:, p, t, h * DH:(h + 1) * DH], Q[:, p, h, t * P:(t + 1) * P],
                                                            start=False, stop=True, skip_group_check=True)
                            last.then_inc(s.o_done, 1)

                        for it in START[:NT]:
                            item(*it)
                        if not first:
                            output_product(s)
                        for it in START[NT:]:
                            item(*it)
                        for l in range(NL):
                            both(0, l)
                            if l >= NL - len(TAIL):
                                item(*TAIL[l - NL + len(TAIL)])
                        for t in range(NT):
                            item("v", t)
                        for i in range(2):
                            within_tiles(0, i)
                            item("r", i)
                        if not final:
                            pe.wait_ge(s.xhat_ready, 1)
                            for t in range(NT):
                                last = nc.tensor.transpose(L[1][:, GT + t * P:GT + (t + 1) * P], XHAT[:, t, :], ident[:, :])
                            last.then_inc(s.xt_done, 1)
                        for i in range(2):
                            key_values(0, i)
                        for it in BEFORE_SECOND:
                            item(*it)
                        for l in range(NL):
                            both(1, l)
                            if l in (NL - 4, NL - 3):
                                from_states(0, l - NL + 4)
                        for i in range(2):
                            within_tiles(1, i)
                            item("r", 2 + i)
                        for i in range(2):
                            key_values(1, i)
                        for i in range(2):
                            from_states(1, i)

                    @block.scalar
                    def _(act):
                        def item(kind, n):
                            if kind == "v" or (kind, n) not in at_item:
                                return
                            i = at_item[kind, n]
                            act.wait_ge(s.proj_done, i + 1)
                            bank = PJ[i % 2]
                            if kind == "k":
                                last = nc.scalar.activation(K[:, n, :], bank[:, :], ACT.Copy)
                            elif kind == "n":
                                if n >= 2:
                                    act.wait_ge(s.sq_read, n - 1)
                                last = nc.scalar.activation(KSQ[:, n % 2, :], bank[:, :], ACT.Square)
                            elif kind == "q":
                                if n >= 2:
                                    act.wait_ge(s.q_one, n - 1)
                                    act.wait_ge(s.lv_done, lv(0, 0, n - 2))
                                for h in range(2):
                                    rows = slice(h * DH, (h + 1) * DH)
                                    last = nc.scalar.activation(Q0[rows, n % 2, h, :], bank[rows, :], ACT.Copy)
                            elif kind == "a":
                                last = nc.scalar.activation(AL[:, n, :], bank[:, :], ACT.Sigmoid, bias=BA[:, n:n + 1])
                            elif kind == "x":
                                last = nc.scalar.activation(XT2[:, :], bank[:, :], ACT.Copy)
                            elif kind == "l":
                                last = nc.scalar.activation(group_of(LG, g - 1), bank[:, 0:NT * E].rearrange("p (t e) -> p t e", e=E), ACT.Copy)
                            else:
                                last = nc.scalar.activation(KTOK[:, n % 2, :, :].rearrange("p t k -> p (t k)"), bank[:, :], ACT.Copy)
                            last.then_inc(s.act_evac, 1)

                        def place(c, l):
                            sz = LEVELS[l]
                            for i in range(2):
                                act.wait_ge(s.lv_done, lv(c, l, i))
                                act.wait_ge(s.merged, mg(c, BLOCKS - 1, i))
                                for b in range(0, P, 2 * sz):
                                    at = BANK[l] * GT
                                    last = nc.scalar.activation(AT[b:b + sz, i, :, b + sz:b + 2 * sz],
                                                                L[i][b:b + sz, at:at + 2 * NT * sz].rearrange("p (n i) -> p n i", i=sz), ACT.Copy)
                                last.then_inc(s.placed, 1)

                        def take_outputs(c, i):
                            act.wait_ge(s.o_done, 2 * c + i + 1)
                            nc.scalar.activation(OT[:, 2 * c + i, :], OB[i][:, :], ACT.Copy).then_inc(s.ot_ready, 1)

                        for it in START:
                            item(*it)
                        for l in range(NL - len(TAIL), NL):
                            if l >= BLOCKS:
                                place(0, l)
                            item(*TAIL[l - NL + len(TAIL)])
                        for it in MIDDLE:
                            item(*it)
                        for it in BEFORE_SECOND:
                            item(*it)
                        if not final:
                            act.wait_ge(s.xn_tmp, 1)
                            nc.scalar.activation(XH[:, 1 - hf, :], XTMP[:, :], ACT.Copy).then_inc(s.xh_ready, 1)
                        take_outputs(0, 0)
                        for l in range(BLOCKS, NL):
                            place(1, l)
                            if l == BLOCKS:
                                take_outputs(0, 1)
                        for it in END:
                            item(*it)
                        for i in range(2):
                            take_outputs(1, i)

                    @block.gpsimd
                    def _(pool):
                        def first_runs(p):
                            pool.wait_ge(s.act_evac, evac("a", p))
                            nc.gpsimd.tensor_tensor(Q[:, p, :, :], Q0[:, p % 2, :, :],
                                                    AL[:, p, :].unsqueeze(1).broadcast_to([P, 2, GT]), ALU.mult).then_inc(s.q_one, 1)

                        def gate_products(c):
                            pair = slice(2 * c, 2 * c + 2)
                            for n, sz in enumerate((2, 4, 8, 16, 32, 64, 128)):
                                src = AL[:, pair, :] if sz == 2 else TT[:, pair, T_AT[sz // 2]:T_AT[sz // 2] + 2 * GT // sz]
                                src = src.rearrange("p n (m two) -> p n m two", two=2)
                                if n:
                                    pool.wait_ge(s.t_ready, 7 * c + n)
                                nc.gpsimd.tensor_tensor(TT[:, pair, T_AT[sz]:T_AT[sz] + GT // sz], src[:, :, :, 0],
                                                        src[:, :, :, 1], ALU.mult).then_inc(s.t_ready, 1)

                        def update(c, l, i):
                            p, sz = 2 * c + i, LEVELS[l]
                            pool.wait_ge(s.lv_done, lv(c, l, i))
                            if sz > 1:
                                pool.wait_ge(s.t_ready, 7 * c + l - 1)
                            q = Q[:, p, :, :].rearrange("p h (m two s) -> p h m two s", two=2, s=sz)[:, :, :, 1, :]
                            t = run_products(p, sz)[:, :, 0].unsqueeze(1).unsqueeze(3).broadcast_to([P, 2, GT // sz // 2, sz])
                            nc.gpsimd.tensor_tensor(q, q, t, ALU.mult).then_inc(s.q_up, 1)

                        norm = norms(s)
                        roots = 0
                        for _ in range(0 if first else 2):
                            roots += 1
                            norm.roots(pool, roots)
                        first_runs(0)
                        first_runs(1)
                        gate_products(0)
                        for l in range(1, NL):
                            for i in range(2):
                                update(0, l, i)
                            if l <= NT:
                                pool.wait_ge(s.n2_ready, 1)
                                nc.gpsimd.tensor_tensor(RN[:, l - 1, :], N2[:, l - 1, :], HALF[:, 0:H], ALU.pow).then_inc(s.rn_ready, 1)
                        if not final:
                            norm.roots(pool, roots + 1)
                        first_runs(2)
                        if not final:
                            norm.roots(pool, roots + 2)
                        first_runs(3)
                        gate_products(1)
                        if not final:
                            pool.wait_ge(s.xh_ready, 1)
                            nc.gpsimd.tensor_tensor(XL[:, 1 - hf, :], XTMP[:, :], XH[:, 1 - hf, :].bitcast(F32), ALU.subtract)
                        for l in range(1, NL):
                            for i in range(2):
                                update(1, l, i)

                    @block.vector
                    def _(v):
                        link, norm = Link(v, s.link), norms(s)

                        def squared_norms():
                            for t in range(NT):
                                v.wait_ge(s.act_evac, evac("n", t))
                                nc.vector.tensor_reduce(N2[:, t, :], KSQ[:, t % 2, :].rearrange("p (h d) -> p h d", d=DH), AX.X, ALU.add).then_inc(s.sq_read, 1)
                            v.wait_ge(s.sq_read, NT)
                            nc.vector.tensor_scalar(N2[:, :, :], N2[:, :, :], NORM_EPS ** 2, None, ALU.max).then_inc(s.n2_ready, 1)

                        def scale_values():
                            for t in range(NT):
                                v.wait_ge(s.rn_ready, t + 1)
                                i = at_item["v", t]
                                v.wait_ge(s.proj_done, i + 1)
                                nc.vector.tensor_tensor(V[:, t, :].rearrange("p (h d) -> p h d", d=DH),
                                                        PJ[i % 2][:, :].rearrange("p (h d) -> p h d", d=DH),
                                                        RN[:, t, :].unsqueeze(2).broadcast_to([P, H, DH]), ALU.mult).then_inc(s.v_scaled, 1)

                        def levels(c):
                            for l, sz in enumerate(LEVELS):
                                for i in range(2):
                                    p = 2 * c + i
                                    v.wait_ge(s.lv_done, lv(c, l, i))
                                    if l:
                                        if sz > 1:
                                            v.wait_ge(s.t_ready, 7 * c + l - 1)
                                        k = K[:, p, :].rearrange("p (m two s) -> p m two s", two=2, s=sz)[:, :, 0, :]
                                        t = run_products(p, sz)[:, :, 1].unsqueeze(2).broadcast_to([P, GT // sz // 2, sz])
                                        nc.vector.tensor_tensor(k, k, t, ALU.mult).then_inc(s.k_up, 1)
                                    if l == 0:
                                        if c:
                                            v.wait_ge(s.within_done, i + 1)
                                        nc.vector.tensor_tensor(AT[:, i, :, :], L[i][:, :].rearrange("p (n i) -> p n i", i=P),
                                                                ident[:, :].unsqueeze(1).broadcast_to([P, 2 * NT, P]), ALU.mult).then_inc(s.merged, 1)
                                    elif l < BLOCKS:
                                        m = P // sz // 2
                                        seconds = lambda ap: ap.rearrange("p n (m two s) -> p n m two s", two=2, s=sz)[:, :, :, 1, :]
                                        got = L[i][:, BANK[l] * GT:(BANK[l] + 1) * GT].rearrange("p (n m s) -> p n m s", m=m, s=sz)
                                        mask = seconds(MASK[:, l - 1, :].unsqueeze(1)).broadcast_to([P, 2 * NT, m, sz])
                                        v.wait_ge(s.merged, mg(c, l - 1, i))
                                        nc.vector.copy_predicated(seconds(AT[:, i, :, :]), mask, got).then_inc(s.merged, 1)

                        def states(c):
                            for i in range(2):
                                p = 2 * c + i
                                v.wait_ge(s.kv_done, p + 1)
                                for t in range(NT):
                                    kv = L[i][:, t * P:(t + 1) * P]
                                    if t:
                                        v.wait_ge(s.s_step, p * NT + t)
                                    if t == 0 and hf == 0:
                                        ins = nc.vector.tensor_copy(S[:, p, 1, :], kv)
                                    else:
                                        ins = nc.vector.scalar_tensor_tensor(S[:, p, t + 1, :], S[:, p, t, :],
                                                                             TT[:, p, T_AT[128] + t:T_AT[128] + t + 1], kv, ALU.mult, ALU.add)
                                    ins.then_inc(s.s_step, 1)

                        squared_norms()
                        if hf:
                            nc.vector.tensor_copy(S[:, :, 0, :], S[:, :, NT, :]).then_inc(s.carried, 1)
                            v.wait_ge(s.carried, 1)
                        if not first:
                            add_residual(v, s, hf)
                            output_norm(v, link, norm, s, g)
                        else:
                            v.wait_ge(load_rest, 16)
                        levels(0)
                        if not final:
                            double_norm(v, link, norm, g + 1, 1 - hf, s.xhat_ready)
                        scale_values()
                        if not final:
                            xt_stage_dve(v, s, s.xn_tmp, L[1][:, GT:])
                        states(0)
                        levels(1)
                        states(1)

            def run_products(p, sz):
                src = AL[:, p, :] if sz == 1 else TT[:, p, T_AT[sz]:T_AT[sz] + GT // sz]
                return src.rearrange("p (m two) -> p m two", two=2)

            def output_product(s):
                for t in range(NT):
                    for p in range(NP_):
                        last = nc.tensor.matmul(OB[0][:, t * P:(t + 1) * P], OT[:, p, t * P:(t + 1) * P], WO[:, p, :],
                                                start=(p == 0), stop=(p == NP_ - 1))
                last.then_inc(s.wo_done, 1)

            def add_residual(v, s, hf):
                v.wait_ge(s.wo_done, 1)
                nc.vector.tensor_tensor(OSUM[:, :, :], OB[0][:, :].rearrange("p (t d) -> p t d", d=D), X1[:, 1 - hf, :, :], ALU.add).then_inc(s.wo_read, 1)
                v.wait_ge(s.wo_read, 1)

            def output_norm(v, link, norm, s, g):
                link(norm(v, link, lambda t: OSUM[:, t, :], lambda t: OSUM[:, t, :]))
                x2 = group_of(X, g - 1)
                link(nc.vector.tensor_tensor(x2, x2, OSUM[:, :, :], ALU.add))
                norm(v, link, lambda t: group_tile(g - 1, t), lambda t: XH2[:, t, :]).then_inc(s.xh2_ready, 1)

            with nc.Block() as block:
                @block.gpsimd
                def _(pool):
                    nc.gpsimd.memset(Q[:, :, :, :], 0.0)

                @block.sync
                def _(sp):
                    clear(sp, A[1])

            attention_block(0, 0, first=True)
            with nc.Fori(0, NG // 2 - 1) as b:
                attention_block(b * 2 + 1, 1)
                attention_block(b * 2 + 2, 0)
            attention_block(NG - 1, 1, final=True)

            with nc.Block() as block:
                s = A[0]

                @block.tensor
                def _(pe):
                    output_product(s)
                    pe.wait_ge(s.xh2_ready, 1)
                    for t in range(NT):
                        last = nc.tensor.transpose(PJ[0][:, t * P:(t + 1) * P], XH2[:, t, :], ident[:, :])
                    last.then_inc(s.xt_done, 1)
                    pe.wait_ge(s.xt2_ready, 1)
                    for t in range(NT):
                        last = nc.tensor.matmul(PJ[1][:, t * E:(t + 1) * E], XT2[:, t * P:(t + 1) * P], GW[:, :], start=True, stop=True)
                    last.then_inc(s.proj_done, 1)

                @block.vector
                def _(v):
                    add_residual(v, s, 0)
                    output_norm(v, Link(v, s.link), norms(s), s, NG)

                @block.gpsimd
                def _(pool):
                    norm = norms(s)
                    norm.roots(pool, 1)
                    norm.roots(pool, 2)

                @block.scalar
                def _(act):
                    act.wait_ge(s.xt_done, 1)
                    nc.scalar.activation(XT2[:, :], PJ[0][:, :], ACT.Copy).then_inc(s.xt2_ready, 1)
                    act.wait_ge(s.proj_done, 1)
                    nc.scalar.activation(group_of(LG, NG - 1), PJ[1][:, 0:NT * E].rearrange("p (t e) -> p t e", e=E), ACT.Copy)

        moe = ExitStack()
        with moe:
            COLS = EF + SF
            GUH = sbuf(moe, "GUH", [P, 2, COLS], F32R)
            GUL = sbuf(moe, "GUL", [P, 2, COLS], F32R)
            GUR = sbuf(moe, "GUR", [P, 2, COLS])
            WD = sbuf(moe, "WD", [P, NF, D])
            CHL = sbuf(moe, "CHL", [P, NG * NT, 2 * E])
            CH = sbuf(moe, "CH", [P, NG * NT, E], F32R)
            W8 = [sbuf(moe, f"W8_{i}", [P, NG * NT, E]) for i in range(4)]
            R1 = [sbuf(moe, f"R1_{i}", [P, NG * NT, 1]) for i in range(4)]
            RANK = sbuf(moe, "RANK", [P, E])
            SELR = sbuf(moe, "SELR", [2 * E, FT, P])
            SEL = sbuf(moe, "SEL", [2 * E, FT, P], F32R)
            CT = sbuf(moe, "CT", [2 * E, 2, GT], F32R)
            SG = sbuf(moe, "SG", [P, 2, GT])
            TU = sbuf(moe, "TU", [P, 2, GT])
            HG = sbuf(moe, "HG", [P, 2, GT])
            G = [moe.enter_context(nc.psum_tensor(f"G{i}", [P, GT], F32)) for i in range(2)]
            U = [moe.enter_context(nc.psum_tensor(f"U{i}", [P, GT], F32)) for i in range(2)]
            C = [moe.enter_context(nc.psum_tensor(f"C{i}", [P, GT], F32)) for i in range(2)]
            Y = [moe.enter_context(nc.psum_tensor(f"Y{i}", [P, GT], F32)) for i in range(2)]
            M = [MoeSems(lambda name: sem(f"m{i}_{name}")) for i in range(2)]

            def norm_next(v, link, norm, s, g):
                norm(v, link, lambda t: tile_of(g, t), lambda t: XHAT[:, t, :]).then_inc(s.xhat_ready, 1)

            def tile_of(g, t):
                if isinstance(g, int):
                    return X[:, g * NT + t, :]
                return X[:, bass.ds(g * NT + t, 1), :].rearrange("p o d -> p (o d)")

            def transpose_next(pe, s, g, slot):
                pe.wait_ge(s.xhat_ready, 1)
                for t in range(NT):
                    last = nc.tensor.transpose(C[0][:, t * P:(t + 1) * P], XHAT[:, t, :], ident[:, :])
                last.then_inc(s.xt_done, 1)
                for t in range(NT):
                    src = CHT[:, t, :]
                    last = nc.tensor.transpose(C[1][0:2 * E, t * P:(t + 1) * P], src, ident[:, :])
                last.then_inc(s.ct_done, 1)

            CHT = sbuf(moe, "CHT", [P, NT, 2 * E])

            def take_next_dve(v, s, slot):
                v.wait_ge(s.xt_done, 1)
                nc.vector.tensor_copy(XTMP[:, :], C[0][:, :]).then_inc(s.xtmp, 1)

            def take_next_act(act, s, slot):
                act.wait_ge(s.ct_done, 1)
                nc.scalar.activation(CT[:, slot, :], C[1][0:2 * E, :], ACT.Copy).then_inc(s.xh_ready, 1)
                act.wait_ge(s.xtmp, 1)
                nc.scalar.activation(XH[:, slot, :], XTMP[:, :], ACT.Copy).then_inc(s.xh_ready, 1)

            def take_next_pool(pool, s, slot):
                pool.wait_ge(s.xh_ready, 2)
                nc.gpsimd.tensor_tensor(XL[:, slot, :], XTMP[:, :], XH[:, slot, :].bitcast(F32), ALU.subtract)

            with nc.Block() as block:
                s = M[0]

                @block.sync
                def _(sp):
                    for i, (we, ws) in enumerate(((w_gate, sw_gate), (w_up, sw_up))):
                        sp.dma_start(GUR[:, i, 0:EF].rearrange("p (e f) -> p e f", f=F), we.rearrange("e d f -> d e f")).then_inc(load_ffn, 16)
                        sp.dma_start(GUR[:, i, EF:], ws).then_inc(load_ffn, 16)
                    sp.dma_start(SELR[:, :, :], c_sel).then_inc(load_ffn, 16)
                    sp.dma_start(RANK[:, :], c_rank).then_inc(load_ffn, 16)
                    sp.dma_start(WD[:, 0:FT, :], w_down.rearrange("e f d -> (e f) d").rearrange("(t p) d -> p t d", p=P)).then_inc(load_ffn, 16)
                    sp.dma_start(WD[:, FT:FT + 2, :], sw_down[0:2 * P, :].rearrange("(t p) d -> p t d", p=P)).then_inc(load_ffn, 16)
                    sp.dma_start(WD[0:SF - 2 * P, FT + 2, :], sw_down[2 * P:SF, :]).then_inc(load_ffn, 16)
                    sp.wait_ge(load_ffn, 9 * 16)

                @block.vector
                def _(v):
                    link = Link(v, s.link)
                    m = lambda r: r[:, :, :].broadcast_to([P, NG * NT, E])
                    rank = RANK[:, :].unsqueeze(1).broadcast_to([P, NG * NT, E])
                    score, work, one, two = (w[:, :, :] for w in W8)
                    top1, top2, aux, tot = (r[:, :, :] for r in R1)
                    tt = lambda o, a, b, op: link(nc.vector.tensor_tensor(o, a, b, op))
                    most = lambda o, a: link(nc.vector.tensor_reduce(o, a, AX.X, ALU.max))
                    norm_next(v, link, norms(s), s, 0)
                    most(aux, LG[:, :, :])
                    nc.vector.tensor_tensor(score, LG[:, :, :], m(R1[2]), ALU.subtract).then_inc(s.exp_in, 1)
                    v.wait_ge(s.exp_done, 1)
                    link(nc.vector.tensor_reduce(tot, score, AX.X, ALU.add))
                    link(nc.vector.reciprocal(tot, tot))
                    tt(score, score, m(R1[3]), ALU.mult)
                    v.wait_ge(load_ffn, 9 * 16)

                    def pick(chosen, best):
                        most(best, score)
                        tt(work, score, best.broadcast_to([P, NG * NT, E]), ALU.is_equal)
                        tt(work, work, rank, ALU.mult)
                        most(aux, work)
                        tt(chosen, work, m(R1[2]), ALU.is_equal)

                    pick(one, top1)
                    link(nc.vector.scalar_tensor_tensor(score, one, -2.0, score, ALU.mult, ALU.add))
                    pick(two, top2)
                    tt(one, one, m(R1[0]), ALU.mult)
                    tt(two, two, m(R1[1]), ALU.mult)
                    tt(one, one, two, ALU.add)
                    tt(tot, top1, top2, ALU.add)
                    link(nc.vector.tensor_scalar(tot, tot, 1e-20, None, ALU.add))
                    link(nc.vector.reciprocal(tot, tot))
                    tt(one, one, m(R1[3]), ALU.mult)
                    link(nc.vector.tensor_scalar(one, one, SCALE, None, ALU.mult))
                    link(nc.vector.tensor_copy(CH[:, :, :], one))
                    nc.vector.tensor_copy(CHL[:, :, 0:E], CH[:, :, :].bitcast(F32))
                    link(nc.vector.tensor_tensor(CHL[:, :, E:], one, CH[:, :, :].bitcast(F32), ALU.subtract))
                    nc.vector.tensor_copy(CHT[:, :, :], CHL[:, 0:NT, :]).then_inc(s.routed, 1)
                    take_next_dve(v, s, 0)

                @block.scalar
                def _(act):
                    act.wait_ge(s.exp_in, 1)
                    nc.scalar.activation(W8[0][:, :, :], W8[0][:, :, :], ACT.Exp).then_inc(s.exp_done, 1)
                    act.wait_ge(load_ffn, 9 * 16)
                    nc.scalar.activation(SEL[:, :, :], SELR[:, :, :], ACT.Copy)
                    for i in range(2):
                        nc.scalar.activation(GUH[:, i, :], GUR[:, i, :], ACT.Copy).then_inc(s.wh_ready, 1)
                    take_next_act(act, s, 0)

                @block.gpsimd
                def _(pool):
                    norms(s).roots(pool, 1)
                    for i in range(2):
                        pool.wait_ge(s.wh_ready, i + 1)
                        nc.gpsimd.tensor_tensor(GUL[:, i, :], GUR[:, i, :], GUH[:, i, :].bitcast(F32), ALU.subtract)
                    take_next_pool(pool, s, 0)

                @block.tensor
                def _(pe):
                    pe.wait_ge(s.routed, 1)
                    transpose_next(pe, s, 0, 0)

            def add_output(v, link, norm, s, g, hf):
                src = lambda t: Y[1 - hf][:, t * P:(t + 1) * P]
                link(norm(v, link, src, lambda t: OSUM[:, t, :]))
                x2 = X[:, bass.ds((g - 1) * NT, NT), :] if not isinstance(g, int) else X[:, (g - 1) * NT:g * NT, :]
                nc.vector.tensor_tensor(x2, x2, OSUM[:, :, :], ALU.add).then_inc(s.x_final, 1)

            def store(sp, s, g):
                sp.wait_ge(s.x_final, 1)
                if isinstance(g, int):
                    sp.dma_start(y_g[:, g - 1, :, :], X[:, (g - 1) * NT:g * NT, :]).then_inc(stored, 16)
                else:
                    sp.dma_start(y_g[:, bass.ds(g - 1, 1), :, :].rearrange("p o t d -> p (o t) d"),
                                 X[:, bass.ds((g - 1) * NT, NT), :]).then_inc(stored, 16)

            def moe_block(g, hf, first=False, final=False):
                s, other = M[1 - hf], M[hf]
                with nc.Block() as block:
                    @block.sync
                    def _(sp):
                        clear(sp, other)
                        if not first:
                            store(sp, s, g)

                    @block.tensor
                    def _(pe):
                        def hidden(f):
                            col, rows = f * P, FTILES[f][1]
                            cols = slice(col, col + rows)
                            if f >= 2:
                                pe.wait_ge(s.silu_done, f - 1)
                            split3(G[f % 2][0:rows, :], GUH[:, 0, cols], GUL[:, 0, cols], XH[:, hf, :], XL[:, hf, :]).then_inc(s.g_done, 1)
                            if f >= 2:
                                pe.wait_ge(s.tu_done, f - 1)
                            last = split3(U[f % 2][0:rows, :], GUH[:, 1, cols], GUL[:, 1, cols], XH[:, hf, :], XL[:, hf, :])
                            if f < FT:
                                if f >= 2:
                                    pe.wait_ge(s.hg_done, f - 1)
                                last = nc.tensor.matmul(C[f % 2][:, :], SEL[:, f, :], CT[:, hf, :], start=True, stop=True)
                            last.then_inc(s.u_done, 1)

                        def down(f):
                            rows = FTILES[f][1]
                            pe.wait_ge(s.hg_done, f + 1)
                            for t in range(NT):
                                last = nc.tensor.matmul(Y[hf][:, t * P:(t + 1) * P], HG[0:rows, f % 2, t * P:(t + 1) * P], WD[0:rows, f, :],
                                                        start=(f == 0 and t == 0), stop=(f == NF - 1), skip_group_check=True)
                            last.then_inc(s.down_done, 1)

                        for f in range(NF):
                            hidden(f)
                            if f == FT + 1 and not final:
                                pe.wait_ge(s.hg_done, FT)
                                transpose_next(pe, s, g + 1, 1 - hf)
                            if f:
                                down(f - 1)
                        down(NF - 1)

                    @block.scalar
                    def _(act):
                        for f, (_, rows) in enumerate(FTILES):
                            act.wait_ge(s.g_done, f + 1)
                            if f >= 2:
                                act.wait_ge(s.tu_done, f - 1)
                            nc.scalar.activation(SG[0:rows, f % 2, :], G[f % 2][0:rows, :], ACT.Silu).then_inc(s.silu_done, 1)
                        if not final:
                            take_next_act(act, s, 1 - hf)

                    @block.gpsimd
                    def _(pool):
                        norm = norms(s)
                        for n in range((0 if first else 1) + (0 if final else 1)):
                            norm.roots(pool, n + 1)
                        if not final:
                            take_next_pool(pool, s, 1 - hf)

                    @block.vector
                    def _(v):
                        link, norm = Link(v, s.link), norms(s)

                        def unit(f):
                            rows = FTILES[f][1]
                            v.wait_ge(s.silu_done, f + 1)
                            v.wait_ge(s.u_done, f + 1)
                            if f >= 2:
                                v.wait_ge(s.down_done, f - 1)
                            if f >= FT:
                                ins = nc.vector.tensor_tensor(HG[0:rows, f % 2, :], SG[0:rows, f % 2, :], U[f % 2][0:rows, :], ALU.mult)
                                ins.then_inc(s.tu_done, 1)
                                v.wait_ge(s.tu_done, f + 1)
                                v.sem_inc(s.hg_done, 1)
                                return
                            nc.vector.tensor_tensor(TU[:, f % 2, :], SG[:, f % 2, :], U[f % 2][:, :], ALU.mult).then_inc(s.tu_done, 1)
                            v.wait_ge(s.tu_done, f + 1)
                            nc.vector.tensor_tensor(HG[:, f % 2, :], TU[:, f % 2, :], C[f % 2][:, :], ALU.mult).then_inc(s.hg_done, 1)

                        for f in range(NF):
                            unit(f)
                            if f == 1 and not first:
                                add_output(v, link, norm, s, g, hf)
                            if f == 3 and not final:
                                src = CHL[:, bass.ds((g + 1) * NT, NT), :] if not isinstance(g, int) else CHL[:, (g + 1) * NT:(g + 2) * NT, :]
                                nc.vector.tensor_copy(CHT[:, :, :], src)
                                norm_next(v, link, norm, s, g + 1)
                        if not final:
                            take_next_dve(v, s, 1 - hf)

            moe_block(0, 0, first=True)
            with nc.Fori(0, NG // 2 - 1) as b:
                moe_block(b * 2 + 1, 1)
                moe_block(b * 2 + 2, 0)
            moe_block(NG - 1, 1, final=True)

            with nc.Block() as block:
                s = M[1]

                @block.vector
                def _(v):
                    add_output(v, Link(v, s.link), norms(s), s, NG, 0)

                @block.gpsimd
                def _(pool):
                    norms(s).roots(pool, 1)

                @block.sync
                def _(sp):
                    store(sp, s, NG)
                    sp.wait_ge(stored, NG * 16)


_INS = ["L0_attn_x", "L0_attn_Wq", "L0_attn_Wk", "L0_attn_Wv", "L0_attn_Wa", "L0_attn_ba", "L0_attn_Wo", "L0_attn_gamma",
        "L0_attn_beta", "L0_ffn_gate_w", "L0_ffn_w_gate", "L0_ffn_w_up", "L0_ffn_w_down", "L0_ffn_sw_gate",
        "L0_ffn_sw_up", "L0_ffn_sw_down"]


def constants():
    import numpy as np

    n = np.arange(P)
    j, i = n[:, None], n[None, :]
    at_level = lambda s: (j // (2 * s) == i // (2 * s)) & (j // s % 2 == 0) & (i // s % 2 == 1)
    masks = np.stack([at_level(1), at_level(2), at_level(4), at_level(8)], axis=1)
    unit_expert = np.arange(EF).reshape(FT, P) // F
    return {
        "ident": np.eye(P, dtype=np.float32),
        "masks": masks.astype(np.uint32),
        "sel": (np.arange(2 * E)[:, None, None] % E == unit_expert[None]).astype(np.float32),
        "rank": np.broadcast_to(np.arange(E, 0, -1, dtype=np.float32), (P, E)).copy(),
    }


def kernel(**inputs):
    import numpy as _np
    import concourse.bacc as _bacc
    from concourse import mybir as _mybir
    from concourse.bass_utils import run_bass_kernel_spmd as _run

    nc = _bacc.Bacc("TRN2", target_bir_lowering=False, num_devices=1)
    arrays, args = {}, []
    given = {f"in_{n}": _np.ascontiguousarray(inputs[n]) for n in _INS}
    for name, a in {**given, **{f"const_{n}": a for n, a in constants().items()}}.items():
        arrays[name] = a
        args.append(nc.dram_tensor(name, a.shape, _mybir.dt.from_np(a.dtype), kind="ExternalInput").ap())
    out = nc.dram_tensor("out_0", (B, SEQ, D), F32, kind="ExternalOutput").ap()
    build(nc, *args, out)
    r = _run(nc, [arrays], core_ids=[0])
    return r.results[0]["out_0"]
```

```python
import concourse.bass as bass
from concourse import mybir
from contextlib import ExitStack

F32 = mybir.dt.float32
F32R = mybir.dt.float32r
U32 = mybir.dt.uint32
ALU = mybir.AluOpType
ACT = mybir.ActivationFunctionType
AX = mybir.AxisListType

B, SEQ, D = 8, 1024, 128
H, DH = 8, 64
P = 128
NT = 4
GT = NT * P
NG = B * SEQ // GT
NP_ = H // 2
SEQ_GROUPS = SEQ // GT
E, F, NS, TOPK, SCALE = 8, 176, 2, 2, 2.5
EF = E * F
FT = EF // P
SF = F * NS
FTILES = [(t, P) for t in range(FT)] + [(FT, P), (FT + 1, P), (FT + 2, SF - 2 * P)]
NF = len(FTILES)
LAG = 3
SPLIT = NF - 2
LN_EPS, NORM_EPS = 1e-5, 1e-12
LEVELS = [0, 1, 2, 4, 8, 16, 32, 64]
BLOCKS = LEVELS.index(16)
BANK = {l: 1 - l % 2 for l in range(1, len(LEVELS))}
T_AT = {2: 0, 4: 256, 8: 384, 16: 448, 32: 480, 64: 496, 128: 504}


class AttentionSems:

    def __init__(self, sem):
        self.link = sem("link")
        self.var_ready = sem("var_ready")
        self.rstd_ready = sem("rstd_ready")
        self.wo_done = sem("wo_done")
        self.wo_read = sem("wo_read")
        self.proj_done = sem("proj_done")
        self.act_evac = sem("act_evac")
        self.sq_read = sem("sq_read")
        self.rn_ready = sem("rn_ready")
        self.v_scaled = sem("v_scaled")
        self.q_one = sem("q_one")
        self.t_ready = sem("t_ready")
        self.x1_ready = sem("x1_ready")
        self.xhat_ready = sem("xhat_ready")
        self.xt_done = sem("xt_done")
        self.xn_tmp = sem("xn_tmp")
        self.xh_ready = sem("xh_ready")
        self.xl_ready = sem("xl_ready")
        self.lv_done = sem("lv_done")
        self.merged = sem("merged")
        self.placed = sem("placed")
        self.q_up = sem("q_up")
        self.q_last = sem("q_last")
        self.k_up = sem("k_up")
        self.carried = sem("carried")
        self.kv_done = sem("kv_done")
        self.s_step = sem("s_step")
        self.within_done = sem("within_done")
        self.o_done = sem("o_done")
        self.ot_ready = sem("ot_ready")
        self.ot_last = sem("ot_last")
        self.xh2_ready = sem("xh2_ready")
        self.all = [self.link, self.var_ready, self.rstd_ready, self.wo_done, self.wo_read, self.proj_done, self.act_evac,
                    self.sq_read, self.rn_ready, self.v_scaled, self.q_one, self.t_ready, self.x1_ready, self.xhat_ready,
                    self.xt_done, self.xn_tmp, self.xh_ready, self.xl_ready, self.lv_done, self.merged, self.placed, self.q_up, self.q_last, self.k_up,
                    self.carried, self.kv_done, self.s_step, self.within_done, self.o_done, self.ot_ready, self.ot_last,
                    self.xh2_ready]


class MoeSems:

    def __init__(self, sem):
        self.link = sem("link")
        self.var_ready = sem("var_ready")
        self.rstd_ready = sem("rstd_ready")
        self.exp_in = sem("exp_in")
        self.exp_done = sem("exp_done")
        self.routed = sem("routed")
        self.xhat_ready = sem("xhat_ready")
        self.xt_done = sem("xt_done")
        self.ct_done = sem("ct_done")
        self.xh_ready = sem("xh_ready")
        self.g_done = sem("g_done")
        self.silu_done = sem("silu_done")
        self.u_done = sem("u_done")
        self.tu_done = sem("tu_done")
        self.y_out = sem("y_out")
        self.y_turned = sem("y_turned")
        self.hgh_done = sem("hgh_done")
        self.hgl_done = sem("hgl_done")
        self.hg_done = sem("hg_done")
        self.down_done = sem("down_done")
        self.normed = sem("normed")
        self.x_final = sem("x_final")
        self.wo_done = sem("wo_done")
        self.wo_read = sem("wo_read")
        self.xh2_ready = sem("xh2_ready")
        self.xt2_done = sem("xt2_done")
        self.xt2_ready = sem("xt2_ready")
        self.logits_done = sem("logits_done")
        self.logits_ready = sem("logits_ready")
        self.all = [self.link, self.var_ready, self.rstd_ready, self.exp_in, self.exp_done, self.routed,
                    self.xhat_ready, self.xt_done, self.ct_done, self.xh_ready, self.g_done, self.silu_done,
                    self.u_done, self.y_out, self.y_turned, self.hgh_done, self.hgl_done,
                    self.tu_done, self.hg_done, self.down_done, self.normed, self.x_final, self.wo_done,
                    self.wo_read, self.xh2_ready, self.xt2_done, self.xt2_ready, self.logits_done, self.logits_ready]


class Link:

    def __init__(self, engine, sem):
        self.engine, self.sem, self.n = engine, sem, 0

    def __call__(self, instruction):
        self.n += 1
        instruction.then_inc(self.sem, 1)
        self.engine.wait_ge(self.sem, self.n)


class Norms:

    def __init__(self, nc, s, st, mv, ve, rs, half):
        self.nc, self.s, self.st, self.mv, self.ve, self.rs, self.half = nc, s, st, mv, ve, rs, half

    def statistics(self, link, lane, src):
        nc, s = self.nc, self.s
        for t in range(NT):
            last = nc.vector.bn_stats(self.st[:, lane, t, :], src(t))
        link(last)
        for t in range(NT):
            last = nc.vector.bn_aggr(self.mv[:, lane, t, :], self.st[:, lane, t, :])
        link(last)
        nc.vector.tensor_scalar(self.ve[:, lane, :], self.mv[:, lane, :, 1], LN_EPS, None, ALU.add).then_inc(s.var_ready, 1)

    def roots(self, pool, counted, lanes):
        pool.wait_ge(self.s.var_ready, counted)
        n, lanes = len(lanes) * NT, slice(lanes[0], lanes[-1] + 1)
        self.nc.gpsimd.tensor_tensor(self.rs[:, lanes, :].rearrange("p l t -> p (l t)"), self.ve[:, lanes, :].rearrange("p l t -> p (l t)"),
                                     self.half[:, 0:n], ALU.pow).then_inc(self.s.rstd_ready, 1)

    def apply(self, v, lane, n, src, dst):
        v.wait_ge(self.s.rstd_ready, n)
        for t in range(NT):
            last = self.nc.vector.tensor_scalar(dst(t), src(t), self.mv[:, lane, t, 0:1], self.rs[:, lane, t:t + 1], ALU.subtract, ALU.mult)
        return last

    def __call__(self, v, link, n, src, dst, lane=0):
        self.statistics(link, lane, src)
        return self.apply(v, lane, n, src, dst)


def build(nc, x, Wq, Wk, Wv, Wa, ba, Wo, gamma, beta, gate_w, w_gate, w_up, w_down, sw_gate, sw_up, sw_down,
          c_ident, c_masks, c_sel, c_rank, y):
    x_g = x.rearrange("b (u t p) d -> p (b u) t d", t=NT, p=P)
    y_g = y.rearrange("b (u t p) d -> p (b u) t d", t=NT, p=P)
    top = ExitStack()
    with top:
        def sbuf(ctx, name, shape, dt=F32):
            return ctx.enter_context(nc.sbuf_tensor(name, shape, dt))

        def sem(name):
            return top.enter_context(nc.semaphore(name))

        def clear(engine, used):
            for s in used.all:
                engine.sem_clear(s)

        X = sbuf(top, "X", [P, NG * NT, D])
        LG = sbuf(top, "LG", [P, NG * NT, E])
        ident = sbuf(top, "ident", [P, P])
        ST = sbuf(top, "ST", [P, 2, NT, 6])
        MV = sbuf(top, "MV", [P, 2, NT, 2])
        VE = sbuf(top, "VE", [P, 2, NT])
        RS = sbuf(top, "RS", [P, 2, NT])
        HALF = sbuf(top, "HALF", [P, NT * H])
        XHAT = sbuf(top, "XHAT", [P, NT, D])
        XH2 = sbuf(top, "XH2", [P, NT, D])
        OSUM = sbuf(top, "OSUM", [P, NT, D])
        X1 = sbuf(top, "X1", [P, 2, NT, D])
        OT = sbuf(top, "OT", [P, NP_, GT])
        WO = sbuf(top, "WO", [P, NP_, D])
        XT2 = sbuf(top, "XT2", [P, GT])
        GW = sbuf(top, "GW", [P, E])
        GUH = sbuf(top, "GUH", [P, 2, EF + SF], F32R)
        GUR = sbuf(top, "GUR", [P, 2, EF + SF])
        WD = sbuf(top, "WD", [P, NF, D])
        RANK = sbuf(top, "RANK", [P, E])
        XTMP = sbuf(top, "XTMP", [P, GT])
        XH = sbuf(top, "XH", [P, 2, GT], F32R)
        XL = sbuf(top, "XL", [P, 2, GT], F32R)

        load_first, load_rest, load_ffn, stored = sem("load_first"), sem("load_rest"), sem("load_ffn"), sem("stored")
        load_w, load_c, load_sel = sem("load_w"), sem("load_c"), sem("load_sel")

        def group_tile(g, t):
            if isinstance(g, int):
                return X[:, g * NT + t, :]
            return X[:, bass.ds(g * NT + t, 1), :].rearrange("p o d -> p (o d)")

        def group_of(tensor, g):
            return tensor[:, bass.ds(g * NT, NT), :] if not isinstance(g, int) else tensor[:, g * NT:(g + 1) * NT, :]

        def norms(s):
            return Norms(nc, s, ST, MV, VE, RS, HALF)

        def split3(out, wh, wl, xh, xl):
            nc.tensor.matmul(out, wl, xh, start=True, stop=False)
            nc.tensor.matmul(out, wh, xl, start=False, stop=False)
            return nc.tensor.matmul(out, wh, xh, start=False, stop=True)

        def output_product(s, bank):
            for t in range(NT):
                for p in range(NP_):
                    last = nc.tensor.matmul(bank[:, t * P:(t + 1) * P], OT[:, p, t * P:(t + 1) * P], WO[:, p, :],
                                            start=(p == 0), stop=(p == NP_ - 1))
            last.then_inc(s.wo_done, 1)

        def add_residual(v, s, bank, slot):
            v.wait_ge(s.wo_done, 1)
            nc.vector.tensor_tensor(OSUM[:, :, :], bank[:, :].rearrange("p (t d) -> p t d", d=D), X1[:, slot, :, :], ALU.add).then_inc(s.wo_read, 1)
            v.wait_ge(s.wo_read, 1)

        att = ExitStack()
        with att:
            WH = sbuf(att, "WH", [P, 4, H * DH], F32R)
            WL = sbuf(att, "WL", [P, 4, H * DH], F32R)
            BA = sbuf(att, "BA", [P, NP_])
            GB = sbuf(att, "GB", [P, 2])
            MASK = sbuf(att, "MASK", [P, 4, P], U32)
            X1N = sbuf(att, "X1N", [P, NT, D])
            Q0 = sbuf(att, "Q0", [P, 2, 2, GT])
            Q = sbuf(att, "Q", [P, NP_, 2, GT])
            K = sbuf(att, "K", [P, NP_, GT])
            KSQ = sbuf(att, "KSQ", [P, 2, GT])
            N2 = sbuf(att, "N2", [P, NT, H])
            RN = sbuf(att, "RN", [P, NT, H])
            AL = sbuf(att, "AL", [P, NP_, GT])
            TT = sbuf(att, "TT", [P, NP_, GT])
            V = sbuf(att, "V", [P, NT, H * DH])
            AT = sbuf(att, "AT", [P, 2, NT * 2, P])
            KTOK = sbuf(att, "KTOK", [P, 2, NT, P])
            S = sbuf(att, "S", [P, NP_, NT + 1, P])
            RAW = Q[:, :, 0, :]
            L = [att.enter_context(nc.psum_tensor(f"L{i}", [P, 2 * NT * P], F32)) for i in range(2)]
            PJ = [att.enter_context(nc.psum_tensor(f"PJ{i}", [P, GT], F32)) for i in range(2)]
            OB = [att.enter_context(nc.psum_tensor(f"OB{i}", [P, GT], F32)) for i in range(2)]

            def take_input(act, s, got, slot):
                nc.scalar.activation(XTMP[:, :], got, ACT.Identity, scale=GB[:, 0:1], bias=GB[:, 1:2]).then_inc(s.xn_tmp, 1)
                act.wait_ge(s.xn_tmp, 1)
                nc.scalar.activation(XH[:, slot, :], XTMP[:, :], ACT.Copy).then_inc(s.xh_ready, 1)

            def input_remainder(pool, s, slot):
                pool.wait_ge(s.xh_ready, 1)
                nc.gpsimd.tensor_tensor(XL[:, slot, :], XTMP[:, :], XH[:, slot, :].bitcast(F32), ALU.subtract).then_inc(s.xl_ready, 1)

            A = [AttentionSems(lambda name: sem(f"a{i}_{name}")) for i in range(2)]

            with nc.Block() as block:
                s = A[0]

                @block.sync
                def _(sp):
                    sp.dma_start(X[:, 0:NT, :], x_g[:, 0, :, :]).then_inc(load_first, 16)
                    for i, w in enumerate((Wq, Wk, Wv, Wa)):
                        sp.dma_start(RAW[:, i, :], w).then_inc(load_w, 16)
                    sp.dma_start(ident[:, :], c_ident).then_inc(load_c, 16)
                    with nc.allow_non_contiguous_dma(reason="small vectors put on partitions"):
                        sp.dma_start(BA[:, :], ba.rearrange("(n p) -> p n", p=P)).then_inc(load_c, 16)
                        sp.dma_start(GB[:, 0:1], gamma.rearrange("(p o) -> p o", o=1)).then_inc(load_c, 16)
                        sp.dma_start(GB[:, 1:2], beta.rearrange("(p o) -> p o", o=1)).then_inc(load_c, 16)
                        sp.dma_start(GW[:, :], gate_w.rearrange("e d -> d e")).then_inc(load_c, 16)
                    sp.dma_start(MASK[:, :, :], c_masks).then_inc(load_c, 16)
                    sp.dma_start(WO[:, :, :], Wo.rearrange("(n p) d -> p n d", p=P)).then_inc(load_c, 16)
                    sp.dma_start(X[:, NT:, :].rearrange("p (g t) d -> p g t d", t=NT), x_g[:, 1:, :, :]).then_inc(load_rest, 16)
                    for i, (we, ws) in enumerate(((w_gate, sw_gate), (w_up, sw_up))):
                        sp.dma_start(GUR[:, i, 0:EF].rearrange("p (e f) -> p e f", f=F), we.rearrange("e d f -> d e f")).then_inc(load_ffn, 16)
                        sp.dma_start(GUR[:, i, EF:], ws).then_inc(load_ffn, 16)
                    sp.dma_start(RANK[:, :], c_rank).then_inc(load_ffn, 16)
                    sp.dma_start(WD[:, 0:FT, :], w_down.rearrange("e f d -> (e f) d").rearrange("(t p) d -> p t d", p=P)).then_inc(load_ffn, 16)
                    sp.dma_start(WD[:, FT:FT + 2, :], sw_down[0:2 * P, :].rearrange("(t p) d -> p t d", p=P)).then_inc(load_ffn, 16)
                    sp.dma_start(WD[0:SF - 2 * P, FT + 2, :], sw_down[2 * P:SF, :]).then_inc(load_ffn, 16)
                    sp.wait_ge(load_c, 7 * 16)

                @block.gpsimd
                def _(pool):
                    nc.gpsimd.memset(HALF[:, :], -0.5).then_inc(s.q_one, 1)
                    nc.gpsimd.memset(Q0[:, :, :, :], 0.0)
                    pool.wait_ge(s.q_one, 1)
                    norm = norms(s)
                    norm.roots(pool, 1, [0])
                    norm.roots(pool, 2, [0])
                    pool.wait_ge(s.act_evac, 1)
                    nc.gpsimd.tensor_tensor(WL[:, :, :], RAW, WH[:, :, :].bitcast(F32), ALU.subtract).then_inc(s.q_up, 1)
                    input_remainder(pool, s, 0)

                @block.scalar
                def _(act):
                    act.wait_ge(load_w, 4 * 16)
                    nc.scalar.activation(WH[:, :, :], RAW, ACT.Copy).then_inc(s.act_evac, 1)
                    act.wait_ge(s.xt_done, 1)
                    take_input(act, s, OB[1][:, :], 0)

                @block.tensor
                def _(pe):
                    pe.wait_ge(load_c, 7 * 16)
                    pe.wait_ge(s.xhat_ready, 1)
                    for t in range(NT):
                        last = nc.tensor.transpose(OB[1][:, t * P:(t + 1) * P], XHAT[:, t, :], ident[:, :])
                    last.then_inc(s.xt_done, 1)

                @block.vector
                def _(v):
                    link, norm = Link(v, s.link), norms(s)
                    v.wait_ge(load_first, 16)
                    x1 = lambda t: X1[:, 0, t, :]
                    link(norm(v, link, 1, lambda t: group_tile(0, t), x1))
                    norm(v, link, 2, x1, lambda t: XHAT[:, t, :]).then_inc(s.xhat_ready, 1)

            FIRST = [[], [("k", 2), ("q", 2)], [("a", 2), ("k", 3)], [("q", 3)], [("a", 3)], [("v", 0), ("v", 1)], [("v", 2)], [("v", 3)]]
            BETWEEN = [("r", 0), ("r", 1), ("t", 0)]
            SECOND = [[("x", 0)], [("l", 0), ("k", 4)], [("q", 4)], [("a", 4)], [("k", 5)], [("q", 5)], [("a", 5)], [("n", 0)]]
            END = [("n", t) for t in range(1, NT)] + [("r", 2), ("r", 3)]
            NEXT = [it for it in sum(SECOND, []) + END if it[0] in "kqan"]
            NL = len(LEVELS)

            def attention_block(g, hf, start=False, first=False, final=False):
                s, other = A[hf], A[1 - hf]
                left_out = lambda it: first and it[0] in "xl" or final and (it in NEXT or it[0] == "t") or start and it not in NEXT
                items = [it for it in sum(FIRST, []) + BETWEEN + sum(SECOND, []) + END if not left_out(it)]
                at_item = {it: i for i, it in enumerate(items)}
                taken = [sum(1 for w, _ in items[:i + 1] if (w == "v") == (items[i][0] == "v")) for i in range(len(items))]
                taken_sem = lambda i: s.v_scaled if items[i][0] == "v" else s.act_evac
                evac = lambda *item: taken[at_item[item]]
                lv = lambda c, l, i: (c * NL + l) * 2 + i + 1
                up = lambda c, l, i: (c * (NL - 1) + l - 1) * 2 + i + 1
                uq = lambda c, l, i: (c * (NL - 2) + l - 1) * 2 + i + 1
                mg = lambda c, l, i: (c * BLOCKS + l) * 2 + i + 1
                pl = lambda c, l, i: (c * (NL - BLOCKS) + l - BLOCKS) * 2 + i + 1

                with nc.Block() as block:
                    @block.sync
                    def _(sp):
                        clear(sp, other)

                    @block.tensor
                    def _(pe):
                        def item(kind, n):
                            if (kind, n) not in at_item:
                                return
                            i = at_item[kind, n]
                            bank = PJ[i % 2]
                            if i >= 2:
                                pe.wait_ge(taken_sem(i - 2), taken[i - 2])
                            x = 1 - hf if kind == "n" or kind in "kqa" and n >= NP_ else hf
                            if x != hf and not start:
                                pe.wait_ge(s.xl_ready, 1)
                            if kind in "kqa":
                                w, p = "qkva".index(kind), n % NP_
                                cols = slice(p * P, (p + 1) * P)
                                last = split3(bank[:, :], WH[:, w, cols], WL[:, w, cols], XH[:, x, :], XL[:, x, :])
                            elif kind in "nv":
                                w, toks = "qkva".index("k" if kind == "n" else "v"), slice(n * P, (n + 1) * P)
                                last = split3(bank[:, :], XH[:, x, toks], XL[:, x, toks], WH[:, w, :], WL[:, w, :])
                            elif kind in "xt":
                                ready, src = (s.xh2_ready, XH2) if kind == "x" else (s.xhat_ready, XHAT)
                                pe.wait_ge(ready, 1)
                                for t in range(NT):
                                    last = nc.tensor.transpose(bank[:, t * P:(t + 1) * P], src[:, t, :], ident[:, :])
                            elif kind == "l":
                                pe.wait_ge(s.act_evac, evac("x", 0))
                                for t in range(NT):
                                    last = nc.tensor.matmul(bank[:, t * E:(t + 1) * E], XT2[:, t * P:(t + 1) * P], GW[:, :],
                                                            start=True, stop=True)
                            else:
                                pe.wait_ge(s.k_up, up(n // 2, NL - 1, n % 2))
                                for t in range(NT):
                                    last = nc.tensor.transpose(bank[:, t * P:(t + 1) * P], K[:, n, t * P:(t + 1) * P], ident[:, :])
                            last.then_inc(s.proj_done, 1)

                        def level(c, l, i):
                            p, sz = 2 * c + i, LEVELS[l]
                            if l == 0:
                                if c:
                                    pe.wait_ge(s.act_evac, evac("q", p))
                                    pe.wait_ge(s.s_step, NT * (i + 1))
                            elif l == 1:
                                if c:
                                    pe.wait_ge(s.q_one, i + 1)
                                pe.wait_ge(s.merged, mg(c, 0, i))
                            else:
                                pe.wait_ge(s.q_up, uq(c, l - 1, i))
                                pe.wait_ge(s.k_up, up(c, l - 1, i))
                                if 2 < l < BLOCKS + 2:
                                    pe.wait_ge(s.merged, mg(c, l - 2, i))
                                elif l >= BLOCKS + 2:
                                    pe.wait_ge(s.placed, pl(c, l - 2, i))
                            for t in range(NT):
                                k = K[:, p, t * P:(t + 1) * P]
                                if l == 0:
                                    last = nc.tensor.matmul(L[i][:, t * 2 * P:(t + 1) * 2 * P], k, Q0[:, i, :, t * P:(t + 1) * P],
                                                            start=True, stop=True)
                                    continue
                                q = Q[:, p, :, t * P:(t + 1) * P]
                                at = BANK[l] * GT
                                if l < BLOCKS:
                                    last = nc.tensor.matmul(L[i][:, at + t * P:at + (t + 1) * P], k,
                                                            q.rearrange("p h (m two s) -> p h m two s", two=2, s=sz)[:, :, :, 1, :],
                                                            start=True, stop=True)
                                    continue
                                for b in range(0, P, 2 * sz):
                                    last = nc.tensor.matmul(L[i][b:b + sz, at + 2 * t * sz:at + 2 * (t + 1) * sz], k[:, b:b + sz],
                                                            q[:, :, b + sz:b + 2 * sz], start=True, stop=True)
                            last.then_inc(s.lv_done, 1)

                        def both(c, l):
                            level(c, l, 0)
                            level(c, l, 1)

                        def within_tiles(c, i):
                            p = 2 * c + i
                            pe.wait_ge(s.merged, mg(c, BLOCKS - 1, i))
                            pe.wait_ge(s.placed, pl(c, NL - 1, i))
                            pe.wait_ge(s.v_scaled, NT)
                            if c:
                                pe.wait_ge(s.ot_ready, i + 1)
                            elif i == 0 and not first:
                                pe.wait_ge(s.wo_read, 1)
                            for t in range(NT):
                                for h in range(2):
                                    last = nc.tensor.matmul(OB[i][h * DH:(h + 1) * DH, t * P:(t + 1) * P],
                                                            V[:, t, (2 * p + h) * DH:(2 * p + h + 1) * DH],
                                                            AT[:, i, 2 * t + h, :], start=(t == 0),
                                                            stop=(hf == 0 and t == 0), skip_group_check=True)
                            last.then_inc(s.within_done, 1)

                        def key_values(c, i):
                            p = 2 * c + i
                            pe.wait_ge(s.act_evac, evac("r", p))
                            for t in range(NT):
                                last = nc.tensor.matmul(L[i][:, t * P:(t + 1) * P], KTOK[:, i, t, :],
                                                        V[:, t, p * P:(p + 1) * P], start=True, stop=True)
                            last.then_inc(s.kv_done, 1)

                        def from_states(c, i):
                            p = 2 * c + i
                            pe.wait_ge(s.q_last, p + 1)
                            for t in range(1 if hf == 0 else 0, NT):
                                if t:
                                    pe.wait_ge(s.s_step, p * NT + t)
                                else:
                                    pe.wait_ge(s.carried, 1)
                                for h in range(2):
                                    last = nc.tensor.matmul(OB[i][h * DH:(h + 1) * DH, t * P:(t + 1) * P],
                                                            S[:, p, t, h * DH:(h + 1) * DH], Q[:, p, h, t * P:(t + 1) * P],
                                                            start=False, stop=True, skip_group_check=True)
                            last.then_inc(s.o_done, 1)

                        if start:
                            for it in items:
                                item(*it)
                            return
                        for l in range(NL):
                            both(0, l)
                            for it in FIRST[l]:
                                item(*it)
                            if l == 0 and not first:
                                pe.wait_ge(s.ot_last, 1)
                                output_product(s, OB[0])
                        for it in BETWEEN[:2]:
                            item(*it)
                        for i in range(2):
                            within_tiles(0, i)
                            key_values(0, i)
                        item(*BETWEEN[2])
                        for l in range(NL):
                            both(1, l)
                            for it in SECOND[l]:
                                item(*it)
                            if l < 2:
                                from_states(0, l)
                        for it in END[:-2]:
                            item(*it)
                        for i in range(2):
                            within_tiles(1, i)
                            item("r", 2 + i)
                        for i in range(2):
                            key_values(1, i)
                        for i in range(2):
                            from_states(1, i)

                    @block.scalar
                    def _(act):
                        def item(kind, n):
                            if kind == "v" or (kind, n) not in at_item:
                                return
                            i = at_item[kind, n]
                            act.wait_ge(s.proj_done, i + 1)
                            bank = PJ[i % 2]
                            if kind == "k":
                                last = nc.scalar.activation(K[:, n % NP_, :], bank[:, :], ACT.Copy)
                            elif kind == "n":
                                if n >= 2:
                                    act.wait_ge(s.sq_read, n - 1)
                                last = nc.scalar.activation(KSQ[:, n % 2, :], bank[:, :], ACT.Square)
                            elif kind == "q":
                                if not start:
                                    act.wait_ge(s.lv_done, lv(n // 2 - 1, 0, n % 2))
                                    if n >= NP_:
                                        act.wait_ge(s.q_one, n - NP_ + 1)
                                for h in range(2):
                                    rows = slice(h * DH, (h + 1) * DH)
                                    last = nc.scalar.activation(Q0[rows, n % 2, h, :], bank[rows, :], ACT.Copy)
                            elif kind == "a":
                                p = n % NP_
                                last = nc.scalar.activation(AL[:, p, :], bank[:, :], ACT.Sigmoid, bias=BA[:, p:p + 1])
                            elif kind == "t":
                                take_input(act, s, bank[:, :], 1 - hf)
                                act.sem_inc(s.act_evac, 1)
                                return
                            elif kind == "x":
                                last = nc.scalar.activation(XT2[:, :], bank[:, :], ACT.Copy)
                            elif kind == "l":
                                last = nc.scalar.activation(group_of(LG, g - 1), bank[:, 0:NT * E].rearrange("p (t e) -> p t e", e=E), ACT.Copy)
                            else:
                                last = nc.scalar.activation(KTOK[:, n % 2, :, :].rearrange("p t k -> p (t k)"), bank[:, :], ACT.Copy)
                            last.then_inc(s.act_evac, 1)

                        def place(c, l):
                            sz = LEVELS[l]
                            for i in range(2):
                                act.wait_ge(s.lv_done, lv(c, l, i))
                                act.wait_ge(s.merged, mg(c, BLOCKS - 1, i))
                                for b in range(0, P, 2 * sz):
                                    at = BANK[l] * GT
                                    last = nc.scalar.activation(AT[b:b + sz, i, :, b + sz:b + 2 * sz],
                                                                L[i][b:b + sz, at:at + 2 * NT * sz].rearrange("p (n i) -> p n i", i=sz), ACT.Copy)
                                last.then_inc(s.placed, 1)

                        def take_outputs(c, i):
                            act.wait_ge(s.o_done, 2 * c + i + 1)
                            nc.scalar.activation(OT[:, 2 * c + i, :], OB[i][:, :], ACT.Copy).then_inc(s.ot_ready, 1)

                        def last_update(c, i):
                            p = 2 * c + i
                            act.wait_ge(s.lv_done, lv(c, NL - 1, i))
                            for t in range(NT):
                                q = Q[:, p, :, t * P + DH:(t + 1) * P]
                                last = nc.scalar.activation(q, q, ACT.Copy, scale=run_products(p, DH)[:, t, 0:1])
                            last.then_inc(s.q_last, 1)

                        if start:
                            for it in items:
                                item(*it)
                            return
                        if not first:
                            nc.scalar.activation(OT[:, NP_ - 1, :], OB[1][:, :], ACT.Copy).then_inc(s.ot_last, 1)
                        for l in range(NL):
                            if l == 2 and not final:
                                act.wait_ge(s.x1_ready, 1)
                                if not first:
                                    act.wait_ge(s.wo_read, 1)
                                nc.scalar.activation(X1[:, 1 - hf, :, :], X1N[:, :, :], ACT.Copy)
                            if l >= BLOCKS:
                                place(0, l)
                            for it in FIRST[l]:
                                item(*it)
                        for it in BETWEEN[:2]:
                            item(*it)
                        for i in range(2):
                            last_update(0, i)
                        item(*BETWEEN[2])
                        for l in range(NL):
                            if l >= BLOCKS:
                                place(1, l)
                            for it in SECOND[l]:
                                item(*it)
                            if l < 2:
                                take_outputs(0, l)
                                if final:
                                    act.wait_ge(load_ffn, 8 * 16)
                                    nc.scalar.activation(GUH[:, l, :], GUR[:, l, :], ACT.Copy)
                        for it in END[:-2]:
                            item(*it)
                        for i in range(2):
                            last_update(1, i)
                            item("r", 2 + i)
                        for i in range(2 if final else 1):
                            take_outputs(1, i)

                    @block.gpsimd
                    def _(pool):
                        def first_runs(p):
                            pool.wait_ge(s.act_evac, evac("a", p))
                            if p >= NP_ and not start:
                                pool.wait_ge(s.o_done, p - NP_ + 1)
                            nc.gpsimd.tensor_tensor(Q[:, p % NP_, :, :], Q0[:, p % 2, :, :],
                                                    AL[:, p % NP_, :].unsqueeze(1).broadcast_to([P, 2, GT]), ALU.mult).then_inc(s.q_one, 1)

                        def gate_products(c):
                            pair = slice(2 * c % NP_, 2 * c % NP_ + 2)
                            before = 7 if c == 2 and not start else 0
                            if before:
                                pool.wait_ge(s.s_step, 2 * NT)
                            for n, sz in enumerate((2, 4, 8, 16, 32, 64, 128)):
                                src = AL[:, pair, :] if sz == 2 else TT[:, pair, T_AT[sz // 2]:T_AT[sz // 2] + 2 * GT // sz]
                                src = src.rearrange("p n (m two) -> p n m two", two=2)
                                if n:
                                    pool.wait_ge(s.t_ready, before + n)
                                nc.gpsimd.tensor_tensor(TT[:, pair, T_AT[sz]:T_AT[sz] + GT // sz], src[:, :, :, 0],
                                                        src[:, :, :, 1], ALU.mult).then_inc(s.t_ready, 1)

                        def update(c, l, i):
                            p, sz = 2 * c + i, LEVELS[l]
                            pool.wait_ge(s.lv_done, lv(c, l, i))
                            if c and sz > 1:
                                pool.wait_ge(s.t_ready, l - 1)
                            q = Q[:, p, :, :].rearrange("p h (m two s) -> p h m two s", two=2, s=sz)[:, :, :, 1, :]
                            t = run_products(p, sz)[:, :, 0].unsqueeze(1).unsqueeze(3).broadcast_to([P, 2, GT // sz // 2, sz])
                            nc.gpsimd.tensor_tensor(q, q, t, ALU.mult).then_inc(s.q_up, 1)

                        def key_norms(t):
                            nc.gpsimd.tensor_tensor(RN[:, t, :], N2[:, t, :], HALF[:, 0:H], ALU.pow).then_inc(s.rn_ready, 1)

                        def prepare_next():
                            for p in (NP_, NP_ + 1):
                                first_runs(p)
                            gate_products(2)

                        if start:
                            prepare_next()
                            return
                        norm = norms(s)
                        key_norms(0)
                        if not final:
                            norm.roots(pool, 1, [1])
                        for t in range(1, NT):
                            key_norms(t)
                        for l in range(1, NL - 1):
                            for i in range(2):
                                update(0, l, i)
                            if l == 1:
                                norm.roots(pool, (0 if first else 1) + (0 if final else 2), ([] if first else [0]) + ([] if final else [1]))
                        first_runs(2)
                        first_runs(3)
                        if not first:
                            norm.roots(pool, 2 if final else 4, [0])
                        gate_products(1)
                        if not final:
                            input_remainder(pool, s, 1 - hf)
                        for l in range(1, NL - 1):
                            for i in range(2):
                                update(1, l, i)
                        if not final:
                            prepare_next()

                    @block.vector
                    def _(v):
                        link, norm = Link(v, s.link), norms(s)

                        def squared_norms():
                            for t in range(NT):
                                v.wait_ge(s.act_evac, evac("n", t))
                                nc.vector.tensor_reduce(N2[:, t, :], KSQ[:, t % 2, :].rearrange("p (h d) -> p h d", d=DH), AX.X, ALU.add).then_inc(s.sq_read, 1)
                            v.wait_ge(s.sq_read, NT)
                            nc.vector.tensor_scalar(N2[:, :, :], N2[:, :, :], NORM_EPS ** 2, None, ALU.max)

                        def scale_values(t):
                            v.wait_ge(s.rn_ready, t + 1)
                            i = at_item["v", t]
                            v.wait_ge(s.proj_done, i + 1)
                            nc.vector.tensor_tensor(V[:, t, :].rearrange("p (h d) -> p h d", d=DH),
                                                    PJ[i % 2][:, :].rearrange("p (h d) -> p h d", d=DH),
                                                    RN[:, t, :].unsqueeze(2).broadcast_to([P, H, DH]), ALU.mult).then_inc(s.v_scaled, 1)

                        x2, xh2 = lambda t: group_tile(g - 1, t), lambda t: XH2[:, t, :]
                        attended = lambda t: OSUM[:, t, :]
                        coming, x1 = lambda t: group_tile(g + 1, t), lambda t: X1N[:, t, :]

                        second = 1 if final else 2

                        def beside(l):
                            for t in ((0, 1) if l == 5 else (2,) if l == 6 else (3,) if l == 7 else ()):
                                scale_values(t)
                            if not final:
                                if l == 0:
                                    norm.apply(v, 1, 1, coming, x1).then_inc(s.x1_ready, 1)
                                    v.wait_ge(s.x1_ready, 1)
                                    norm.statistics(link, 1, x1)
                            if not first:
                                if l == 0:
                                    add_residual(v, s, OB[0], 1 - hf)
                                    norm.statistics(link, 0, attended)
                                elif l == 4:
                                    link(norm.apply(v, 0, second, attended, attended))
                                elif l == 6:
                                    link(nc.vector.tensor_tensor(group_of(X, g - 1), group_of(X, g - 1), OSUM[:, :, :], ALU.add))
                                elif l == 7:
                                    norm.statistics(link, 0, x2)

                        def levels(c):
                            for l, sz in enumerate(LEVELS):
                                for i in range(2):
                                    p = 2 * c + i
                                    v.wait_ge(s.lv_done, lv(c, l, i))
                                    if l:
                                        if c and sz > 1:
                                            v.wait_ge(s.t_ready, l - 1)
                                        k = K[:, p, :].rearrange("p (m two s) -> p m two s", two=2, s=sz)[:, :, 0, :]
                                        t = run_products(p, sz)[:, :, 1].unsqueeze(2).broadcast_to([P, GT // sz // 2, sz])
                                        nc.vector.tensor_tensor(k, k, t, ALU.mult).then_inc(s.k_up, 1)
                                    if l == 0:
                                        if c:
                                            v.wait_ge(s.within_done, i + 1)
                                        nc.vector.tensor_tensor(AT[:, i, :, :], L[i][:, :].rearrange("p (n i) -> p n i", i=P),
                                                                ident[:, :].unsqueeze(1).broadcast_to([P, 2 * NT, P]), ALU.mult).then_inc(s.merged, 1)
                                    elif l < BLOCKS:
                                        m = P // sz // 2
                                        seconds = lambda ap: ap.rearrange("p n (m two s) -> p n m two s", two=2, s=sz)[:, :, :, 1, :]
                                        got = L[i][:, BANK[l] * GT:(BANK[l] + 1) * GT].rearrange("p (n m s) -> p n m s", m=m, s=sz)
                                        mask = seconds(MASK[:, l - 1, :].unsqueeze(1)).broadcast_to([P, 2 * NT, m, sz])
                                        v.wait_ge(s.merged, mg(c, l - 1, i))
                                        nc.vector.copy_predicated(seconds(AT[:, i, :, :]), mask, got).then_inc(s.merged, 1)
                                if c == 0:
                                    beside(l)

                        def states(c):
                            for i in range(2):
                                p = 2 * c + i
                                v.wait_ge(s.kv_done, p + 1)
                                for t in range(NT):
                                    kv = L[i][:, t * P:(t + 1) * P]
                                    if t:
                                        v.wait_ge(s.s_step, p * NT + t)
                                    if t == 0 and hf == 0:
                                        ins = nc.vector.tensor_copy(S[:, p, 1, :], kv)
                                    else:
                                        ins = nc.vector.scalar_tensor_tensor(S[:, p, t + 1, :], S[:, p, t, :],
                                                                             TT[:, p, T_AT[128] + t:T_AT[128] + t + 1], kv, ALU.mult, ALU.add)
                                    ins.then_inc(s.s_step, 1)

                        if start:
                            squared_norms()
                            return
                        if hf:
                            nc.vector.tensor_copy(S[:, :, 0, :], S[:, :, NT, :]).then_inc(s.carried, 1)
                            v.wait_ge(s.carried, 1)
                        if first:
                            v.wait_ge(load_rest, 16)
                        if not final:
                            norm.statistics(link, 1, coming)
                        levels(0)
                        if not final:
                            norm.apply(v, 1, second, x1, lambda t: XHAT[:, t, :]).then_inc(s.xhat_ready, 1)
                        states(0)
                        if not first:
                            norm.apply(v, 0, second + 1, x2, xh2).then_inc(s.xh2_ready, 1)
                        levels(1)
                        if not final:
                            squared_norms()
                        states(1)

            def run_products(p, sz):
                src = AL[:, p, :] if sz == 1 else TT[:, p, T_AT[sz]:T_AT[sz] + GT // sz]
                return src.rearrange("p (m two) -> p m two", two=2)

            attention_block(-1, 1, start=True)
            attention_block(0, 0, first=True)
            with nc.Fori(0, NG // 2 - 1) as b:
                attention_block(b * 2 + 1, 1)
                attention_block(b * 2 + 2, 0)
            attention_block(NG - 1, 1, final=True)

        moe = ExitStack()
        with moe:
            GUL = sbuf(moe, "GUL", [P, 2, EF + SF], F32R)
            CHT = sbuf(moe, "CHT", [P, NT, 2 * E])
            CH = sbuf(moe, "CH", [P, NT, E], F32R)
            W8 = [sbuf(moe, f"W8_{i}", [P, NT, E]) for i in range(4)]
            R1 = [sbuf(moe, f"R1_{i}", [P, NT, 1]) for i in range(4)]
            SELR = sbuf(moe, "SELR", [2 * E, FT, P])
            LMAX = sbuf(moe, "LMAX", [P, NG * NT, 1])
            SEL = sbuf(moe, "SEL", [2 * E, FT, P], F32R)
            CT = sbuf(moe, "CT", [2 * E, 2, GT], F32R)
            SG = sbuf(moe, "SG", [P, 2, GT])
            TU = sbuf(moe, "TU", [P, 2, GT])
            HG = sbuf(moe, "HG", [P, LAG + 1, GT])
            HGH = sbuf(moe, "HGH", [P, LAG + 1, GT], F32R)
            HGL = sbuf(moe, "HGL", [P, LAG + 1, GT], F32R)
            WDH = sbuf(moe, "WDH", [P, SPLIT, D], F32R)
            WDL = sbuf(moe, "WDL", [P, SPLIT, D], F32R)
            YS = sbuf(moe, "YS", [P, GT])
            G = [moe.enter_context(nc.psum_tensor(f"G{i}", [P, GT], F32)) for i in range(2)]
            U = [moe.enter_context(nc.psum_tensor(f"U{i}", [P, GT], F32)) for i in range(2)]
            C = [moe.enter_context(nc.psum_tensor(f"C{i}", [P, GT], F32)) for i in range(2)]
            Y = [moe.enter_context(nc.psum_tensor(f"Y{i}", [P, GT], F32)) for i in range(2)]
            M = [MoeSems(lambda name: sem(f"m{i}_{name}")) for i in range(2)]

            score, work, one, two = (w[:, :, :] for w in W8)
            top1, top2, aux, tot = (r[:, :, :] for r in R1)
            PARTS = 5

            def route(link, part, g, done):
                tt = lambda out, a, b, op: link(nc.vector.tensor_tensor(out, a, b, op))
                most = lambda out, a: link(nc.vector.tensor_reduce(out, a, AX.X, ALU.max))
                wide = lambda r: r.broadcast_to([P, NT, E])
                rank = RANK[:, :].unsqueeze(1).broadcast_to([P, NT, E])

                def candidates(best):
                    most(best, score)
                    tt(work, score, wide(best), ALU.is_equal)
                    tt(work, work, rank, ALU.mult)

                def choose(chosen):
                    most(aux, work)
                    tt(chosen, work, wide(aux), ALU.is_equal)

                if part == 0:
                    link(nc.vector.tensor_reduce(tot, group_of(LG, g), AX.X, ALU.add))
                    link(nc.vector.reciprocal(tot, tot))
                    tt(score, group_of(LG, g), wide(tot), ALU.mult)
                elif part == 1:
                    candidates(top1)
                    choose(one)
                elif part == 2:
                    link(nc.vector.scalar_tensor_tensor(score, one, -2.0, score, ALU.mult, ALU.add))
                    candidates(top2)
                elif part == 3:
                    choose(two)
                    tt(tot, top1, top2, ALU.add)
                    link(nc.vector.tensor_scalar(tot, tot, 1e-20, None, ALU.add))
                    link(nc.vector.reciprocal(tot, tot))
                else:
                    tt(one, one, wide(top1), ALU.mult)
                    tt(two, two, wide(top2), ALU.mult)
                    tt(one, one, two, ALU.add)
                    link(nc.vector.scalar_tensor_tensor(one, one, SCALE, wide(tot), ALU.mult, ALU.mult))
                    link(nc.vector.tensor_copy(CH[:, :, :], one))
                    nc.vector.tensor_copy(CHT[:, :, 0:E], CH[:, :, :].bitcast(F32))
                    nc.vector.tensor_tensor(CHT[:, :, E:], one, CH[:, :, :].bitcast(F32), ALU.subtract).then_inc(done, 1)

            def transpose_input(pe, s):
                pe.wait_ge(s.xhat_ready, 1)
                for t in range(NT):
                    last = nc.tensor.transpose(C[0][:, t * P:(t + 1) * P], XHAT[:, t, :], ident[:, :])
                last.then_inc(s.xt_done, 1)

            def transpose_routing(pe, s):
                pe.wait_ge(s.routed, 1)
                for t in range(NT):
                    last = nc.tensor.transpose(C[1][0:2 * E, t * P:(t + 1) * P], CHT[:, t, :], ident[:, :])
                last.then_inc(s.ct_done, 1)

            def take_next_act(act, s, slot):
                act.wait_ge(s.xt_done, 1)
                nc.scalar.activation(XH[:, slot, :], C[0][:, :], ACT.Copy).then_inc(s.xh_ready, 1)
                act.wait_ge(s.ct_done, 1)
                nc.scalar.activation(CT[:, slot, :], C[1][0:2 * E, :], ACT.Copy)

            def take_next_dve(v, s, slot):
                v.wait_ge(s.xh_ready, 1)
                nc.vector.tensor_tensor(XL[:, slot, :], C[0][:, :], XH[:, slot, :].bitcast(F32), ALU.subtract)

            def centre(link, tiles, done):
                link(nc.vector.tensor_reduce(LMAX[:, tiles, :], LG[:, tiles, :], AX.X, ALU.max))
                n = tiles.stop - tiles.start
                nc.vector.tensor_tensor(LG[:, tiles, :], LG[:, tiles, :], LMAX[:, tiles, :].broadcast_to([P, n, E]), ALU.subtract).then_inc(done, 1)

            BUT_LAST, LAST = slice(0, (NG - 1) * NT), slice((NG - 1) * NT, NG * NT)

            with nc.Block() as block:
                s = M[0]

                @block.sync
                def _(sp):
                    sp.dma_start(SELR[:, :, :], c_sel).then_inc(load_sel, 16)

                @block.vector
                def _(v):
                    link = Link(v, s.link)
                    centre(link, BUT_LAST, s.exp_in)
                    nc.vector.tensor_tensor(GUL[:, 1, :], GUR[:, 1, :], GUH[:, 1, :].bitcast(F32), ALU.subtract)
                    norms(s)(v, link, 1, lambda t: group_tile(0, t), lambda t: XHAT[:, t, :]).then_inc(s.xhat_ready, 1)
                    v.wait_ge(s.exp_done, 1)
                    v.wait_ge(load_ffn, 8 * 16)
                    for part in range(PARTS):
                        route(link, part, 0, s.routed)
                    take_next_dve(v, s, 0)

                @block.scalar
                def _(act):
                    act.wait_ge(s.exp_in, 1)
                    nc.scalar.activation(LG[:, BUT_LAST, :], LG[:, BUT_LAST, :], ACT.Exp).then_inc(s.exp_done, 1)
                    act.wait_ge(load_sel, 16)
                    nc.scalar.activation(SEL[:, :, :], SELR[:, :, :], ACT.Copy)
                    nc.scalar.activation(WDH[:, :, :], WD[:, 0:SPLIT, :], ACT.Copy)
                    take_next_act(act, s, 0)

                @block.gpsimd
                def _(pool):
                    nc.gpsimd.tensor_tensor(GUL[:, 0, :], GUR[:, 0, :], GUH[:, 0, :].bitcast(F32), ALU.subtract)
                    norms(s).roots(pool, 1, [0])

                @block.tensor
                def _(pe):
                    transpose_input(pe, s)
                    transpose_routing(pe, s)

            def store(sp, s, g):
                sp.wait_ge(s.x_final, 1)
                if isinstance(g, int):
                    sp.dma_start(y_g[:, g - 1, :, :], X[:, (g - 1) * NT:g * NT, :]).then_inc(stored, 16)
                else:
                    sp.dma_start(y_g[:, bass.ds(g - 1, 1), :, :].rearrange("p o t d -> p (o t) d"),
                                 X[:, bass.ds((g - 1) * NT, NT), :]).then_inc(stored, 16)

            def moe_block(g, hf, first=False, final=False):
                s, other = M[1 - hf], M[hf]
                spare = Y[1 - hf]
                with nc.Block() as block:
                    @block.sync
                    def _(sp):
                        clear(sp, other)
                        if not first:
                            store(sp, s, g)

                    @block.tensor
                    def _(pe):
                        def hidden(f):
                            col, rows = f * P, FTILES[f][1]
                            cols = slice(col, col + rows)
                            if f >= 2:
                                pe.wait_ge(s.silu_done, f - 1)
                            split3(G[f % 2][0:rows, :], GUH[:, 0, cols], GUL[:, 0, cols], XH[:, hf, :], XL[:, hf, :]).then_inc(s.g_done, 1)
                            if f >= 2:
                                pe.wait_ge(s.tu_done, f - 1)
                            last = split3(U[f % 2][0:rows, :], GUH[:, 1, cols], GUL[:, 1, cols], XH[:, hf, :], XL[:, hf, :])
                            if f < FT:
                                if f >= 2:
                                    pe.wait_ge(s.hg_done, f - 1)
                                last = nc.tensor.matmul(C[f % 2][:, :], SEL[:, f, :], CT[:, hf, :], start=True, stop=True)
                            last.then_inc(s.u_done, 1)

                        def down(f):
                            rows = FTILES[f][1]
                            out = Y[hf][:, :]
                            if f >= SPLIT:
                                pe.wait_ge(s.hg_done, f + 1)
                                nc.tensor.matmul(out, WD[0:rows, f, :], HG[0:rows, f % (LAG + 1), :], start=False, stop=(f == NF - 1)).then_inc(s.down_done, 1)
                                return
                            pe.wait_ge(s.hgl_done, f + 1)
                            nc.tensor.matmul(out, WDL[:, f, :], HGH[:, f % (LAG + 1), :], start=(f == 0), stop=False)
                            nc.tensor.matmul(out, WDH[:, f, :], HGL[:, f % (LAG + 1), :], start=False, stop=False)
                            nc.tensor.matmul(out, WDH[:, f, :], HGH[:, f % (LAG + 1), :], start=False, stop=False).then_inc(s.down_done, 1)

                        for f in range(NF):
                            hidden(f)
                            if f == 1 and not first:
                                turn_output(pe, s, spare)
                            if f >= LAG:
                                down(f - LAG)
                            if f == FT + 1 and not final:
                                pe.wait_ge(s.hg_done, FT)
                                transpose_input(pe, s)
                            if f == NF - 1 and not final:
                                transpose_routing(pe, s)
                            if first and f == 1:
                                output_product(s, spare)
                            if first and f == 9:
                                pe.wait_ge(s.xh2_ready, 1)
                                for t in range(NT):
                                    last = nc.tensor.transpose(spare[:, t * P:(t + 1) * P], XH2[:, t, :], ident[:, :])
                                last.then_inc(s.xt2_done, 1)
                            if first and f == 10:
                                pe.wait_ge(s.xt2_ready, 1)
                                for t in range(NT):
                                    last = nc.tensor.matmul(spare[:, t * E:(t + 1) * E], XT2[:, t * P:(t + 1) * P], GW[:, :], start=True, stop=True)
                                last.then_inc(s.logits_done, 1)
                        for f in range(NF - LAG, NF):
                            down(f)

                    @block.scalar
                    def _(act):
                        if not first:
                            take_output(s, spare)
                        for f, (_, rows) in enumerate(FTILES):
                            act.wait_ge(s.g_done, f + 1)
                            if f >= 2:
                                act.wait_ge(s.tu_done, f - 1)
                            nc.scalar.activation(SG[0:rows, f % 2, :], G[f % 2][0:rows, :], ACT.Silu).then_inc(s.silu_done, 1)
                            if 1 <= f <= SPLIT:
                                act.wait_ge(s.hg_done, f)
                                if f > LAG + 1:
                                    act.wait_ge(s.down_done, f - LAG - 1)
                                nc.scalar.activation(HGH[:, (f - 1) % (LAG + 1), :], HG[:, (f - 1) % (LAG + 1), :], ACT.Copy).then_inc(s.hgh_done, 1)
                            if first and f == 9:
                                act.wait_ge(s.xt2_done, 1)
                                nc.scalar.activation(XT2[:, :], spare[:, :], ACT.Copy).then_inc(s.xt2_ready, 1)
                            if first and f == 10:
                                act.wait_ge(s.logits_done, 1)
                                nc.scalar.activation(LG[:, LAST, :], spare[:, 0:NT * E].rearrange("p (t e) -> p t e", e=E), ACT.Copy).then_inc(s.logits_ready, 1)
                            if f == FT + 1 and not final:
                                take_next_act(act, s, 1 - hf)
                        if first:
                            act.wait_ge(s.exp_in, 1)
                            nc.scalar.activation(LG[:, LAST, :], LG[:, LAST, :], ACT.Exp)

                    @block.gpsimd
                    def _(pool):
                        norm = norms(s)
                        if first:
                            nc.gpsimd.tensor_tensor(WDL[:, :, :], WD[:, 0:SPLIT, :], WDH[:, :, :].bitcast(F32), ALU.subtract)
                        for f in range(SPLIT):
                            pool.wait_ge(s.hgh_done, f + 1)
                            if f > LAG:
                                pool.wait_ge(s.down_done, f - LAG)
                            nc.gpsimd.tensor_tensor(HGL[:, f % (LAG + 1), :], HG[:, f % (LAG + 1), :], HGH[:, f % (LAG + 1), :].bitcast(F32), ALU.subtract).then_inc(s.hgl_done, 1)
                            if first:
                                if f == 0:
                                    norm.roots(pool, 1, [1])
                                elif f == 2:
                                    norm.roots(pool, 2, [0])
                                elif f == 4:
                                    add_normed(pool, s, NG)
                                elif f == 6:
                                    norm.roots(pool, 3, [0])
                            else:
                                if f == 2:
                                    norm.roots(pool, 1 if final else 2, [0] if final else [0, 1])
                                elif f == 4:
                                    add_normed(pool, s, g)

                    @block.vector
                    def _(v):
                        link, norm = Link(v, s.link), norms(s)

                        def unit(f):
                            rows = FTILES[f][1]
                            v.wait_ge(s.silu_done, f + 1)
                            v.wait_ge(s.u_done, f + 1)
                            if LAG < f < SPLIT + LAG + 1:
                                v.wait_ge(s.hgl_done, f - LAG)
                            if f >= FT:
                                ins = nc.vector.tensor_tensor(HG[0:rows, f % (LAG + 1), :], SG[0:rows, f % 2, :], U[f % 2][0:rows, :], ALU.mult)
                                ins.then_inc(s.tu_done, 1)
                                v.wait_ge(s.tu_done, f + 1)
                                v.sem_inc(s.hg_done, 1)
                                return
                            nc.vector.tensor_tensor(TU[:, f % 2, :], SG[:, f % 2, :], U[f % 2][:, :], ALU.mult).then_inc(s.tu_done, 1)
                            v.wait_ge(s.tu_done, f + 1)
                            nc.vector.tensor_tensor(HG[:, f % (LAG + 1), :], TU[:, f % 2, :], C[f % 2][:, :], ALU.mult).then_inc(s.hg_done, 1)

                        coming, attended = lambda t: group_tile(g + 1, t), lambda t: OSUM[:, t, :]
                        made = lambda t: spare[:, t * P:(t + 1) * P]
                        for f in range(NF):
                            unit(f)
                            if not final:
                                if f == (1 if first else 2):
                                    norm.statistics(link, 1, coming)
                                elif f == 6:
                                    norm.apply(v, 1, 1, coming, lambda t: XHAT[:, t, :]).then_inc(s.xhat_ready, 1)
                                elif 7 <= f < 7 + PARTS:
                                    route(link, f - 7, g + 1, s.routed)
                                elif f == NF - 1:
                                    take_next_dve(v, s, 1 - hf)
                            if not first:
                                if f == 1:
                                    v.wait_ge(s.y_turned, 1)
                                    norm.statistics(link, 0, made)
                                elif f == 5:
                                    norm.apply(v, 0, 1, made, attended).then_inc(s.normed, 1)
                            else:
                                if f == 2:
                                    add_residual(v, s, spare, (NG - 1) % 2)
                                    norm.statistics(link, 0, attended)
                                elif f == 4:
                                    norm.apply(v, 0, 2, attended, attended).then_inc(s.normed, 1)
                                elif f == 6:
                                    v.wait_ge(s.x_final, 1)
                                    norm.statistics(link, 0, lambda t: group_tile(NG - 1, t))
                                elif f == 8:
                                    norm.apply(v, 0, 3, lambda t: group_tile(NG - 1, t), lambda t: XH2[:, t, :]).then_inc(s.xh2_ready, 1)
                                elif f == FT:
                                    v.wait_ge(s.logits_ready, 1)
                                    centre(link, LAST, s.exp_in)

            def take_output(s, bank):
                nc.scalar.activation(YS[:, :], bank[:, :], ACT.Copy).then_inc(s.y_out, 1)

            def turn_output(pe, s, bank):
                pe.wait_ge(s.y_out, 1)
                for t in range(NT):
                    last = nc.tensor.transpose(bank[:, t * P:(t + 1) * P], YS[:, t * P:(t + 1) * P], ident[:, :])
                last.then_inc(s.y_turned, 1)

            def add_normed(pool, s, g):
                pool.wait_ge(s.normed, 1)
                x = group_of(X, g - 1)
                nc.gpsimd.tensor_tensor(x, x, OSUM[:, :, :], ALU.add).then_inc(s.x_final, 1)

            moe_block(0, 0, first=True)
            with nc.Fori(0, NG // 2 - 1) as b:
                moe_block(b * 2 + 1, 1)
                moe_block(b * 2 + 2, 0)
            moe_block(NG - 1, 1, final=True)

            with nc.Block() as block:
                s = M[1]

                @block.scalar
                def _(act):
                    take_output(s, Y[1])

                @block.tensor
                def _(pe):
                    turn_output(pe, s, Y[1])

                @block.vector
                def _(v):
                    v.wait_ge(s.y_turned, 1)
                    norms(s)(v, Link(v, s.link), 1, lambda t: Y[1][:, t * P:(t + 1) * P], lambda t: OSUM[:, t, :]).then_inc(s.normed, 1)
                    v.wait_ge(s.normed, 1)
                    nc.vector.tensor_tensor(group_of(X, NG - 1), group_of(X, NG - 1), OSUM[:, :, :], ALU.add).then_inc(s.x_final, 1)

                @block.gpsimd
                def _(pool):
                    norms(s).roots(pool, 1, [0])

                @block.sync
                def _(sp):
                    store(sp, s, NG)
                    sp.wait_ge(stored, NG * 16)


_INS = ["L0_attn_x", "L0_attn_Wq", "L0_attn_Wk", "L0_attn_Wv", "L0_attn_Wa", "L0_attn_ba", "L0_attn_Wo", "L0_attn_gamma",
        "L0_attn_beta", "L0_ffn_gate_w", "L0_ffn_w_gate", "L0_ffn_w_up", "L0_ffn_w_down", "L0_ffn_sw_gate",
        "L0_ffn_sw_up", "L0_ffn_sw_down"]


def constants():
    import numpy as np

    n = np.arange(P)
    j, i = n[:, None], n[None, :]
    at_level = lambda s: (j // (2 * s) == i // (2 * s)) & (j // s % 2 == 0) & (i // s % 2 == 1)
    masks = np.stack([at_level(1), at_level(2), at_level(4), at_level(8)], axis=1)
    unit_expert = np.arange(EF).reshape(FT, P) // F
    return {
        "ident": np.eye(P, dtype=np.float32),
        "masks": masks.astype(np.uint32),
        "sel": (np.arange(2 * E)[:, None, None] % E == unit_expert[None]).astype(np.float32),
        "rank": np.broadcast_to(np.arange(E, 0, -1, dtype=np.float32), (P, E)).copy(),
    }


def kernel(**inputs):
    import numpy as _np
    import concourse.bacc as _bacc
    from concourse import mybir as _mybir
    from concourse.bass_utils import run_bass_kernel_spmd as _run

    nc = _bacc.Bacc("TRN2", target_bir_lowering=False, num_devices=1)
    arrays, args = {}, []
    given = {f"in_{n}": _np.ascontiguousarray(inputs[n]) for n in _INS}
    for name, a in {**given, **{f"const_{n}": a for n, a in constants().items()}}.items():
        arrays[name] = a
        args.append(nc.dram_tensor(name, a.shape, _mybir.dt.from_np(a.dtype), kind="ExternalInput").ap())
    out = nc.dram_tensor("out_0", (B, SEQ, D), F32, kind="ExternalOutput").ap()
    build(nc, *args, out)
    r = _run(nc, [arrays], core_ids=[0])
    return r.results[0]["out_0"]
```

```python
import concourse.bass as bass
from concourse import mybir
from contextlib import ExitStack

F32 = mybir.dt.float32
F32R = mybir.dt.float32r
U32 = mybir.dt.uint32
ALU = mybir.AluOpType
ACT = mybir.ActivationFunctionType
AX = mybir.AxisListType

B, SEQ, D = 8, 1024, 128
H, DH = 8, 64
P = 128
NT = 4
GT = NT * P
NG = B * SEQ // GT
NP_ = H // 2
SEQ_GROUPS = SEQ // GT
E, F, NS, TOPK, SCALE = 8, 176, 2, 2, 2.5
EF = E * F
FT = EF // P
SF = F * NS
FTILES = [(t, P) for t in range(FT)] + [(FT, P), (FT + 1, P), (FT + 2, SF - 2 * P)]
NF = len(FTILES)
LAG = 3
SPLIT = NF - 2
LN_EPS, NORM_EPS = 1e-5, 1e-12
LEVELS = [0, 1, 2, 4, 8, 16, 32, 64]
BLOCKS = LEVELS.index(16)
BANK = {l: 1 - l % 2 for l in range(1, len(LEVELS))}
T_AT = {2: 0, 4: 256, 8: 384, 16: 448, 32: 480, 64: 496, 128: 504}


class AttentionSems:

    def __init__(self, sem):
        self.link = sem("link")
        self.var_ready = sem("var_ready")
        self.rstd_ready = sem("rstd_ready")
        self.wo_done = sem("wo_done")
        self.wo_read = sem("wo_read")
        self.proj_done = sem("proj_done")
        self.act_evac = sem("act_evac")
        self.qt_read = sem("qt_read")
        self.sq_read = sem("sq_read")
        self.rn_ready = sem("rn_ready")
        self.v_scaled = sem("v_scaled")
        self.q_one = sem("q_one")
        self.t_ready = sem("t_ready")
        self.x1_ready = sem("x1_ready")
        self.xhat_ready = sem("xhat_ready")
        self.xt_done = sem("xt_done")
        self.xn_tmp = sem("xn_tmp")
        self.xh_ready = sem("xh_ready")
        self.xl_ready = sem("xl_ready")
        self.lv_done = sem("lv_done")
        self.based = sem("based")
        self.based_act = sem("based_act")
        self.merged = sem("merged")
        self.placed = sem("placed")
        self.q_two = sem("q_two")
        self.q_up = sem("q_up")
        self.q_last = sem("q_last")
        self.k_up = sem("k_up")
        self.carried = sem("carried")
        self.kv_done = sem("kv_done")
        self.s_step = sem("s_step")
        self.within_done = sem("within_done")
        self.o_done = sem("o_done")
        self.ot_ready = sem("ot_ready")
        self.ot_last = sem("ot_last")
        self.xh2_ready = sem("xh2_ready")
        self.exp_in = sem("exp_in")
        self.exp_done = sem("exp_done")
        self.routed = sem("routed")
        self.all = [self.link, self.var_ready, self.rstd_ready, self.wo_done, self.wo_read, self.proj_done, self.act_evac,
                    self.sq_read, self.qt_read, self.rn_ready, self.v_scaled, self.q_one, self.t_ready, self.x1_ready, self.xhat_ready,
                    self.xt_done, self.xn_tmp, self.xh_ready, self.xl_ready, self.lv_done, self.based, self.based_act, self.merged, self.placed, self.q_two, self.q_up, self.q_last, self.k_up,
                    self.carried, self.kv_done, self.s_step, self.within_done, self.o_done, self.ot_ready, self.ot_last,
                    self.xh2_ready, self.exp_in, self.exp_done, self.routed]


class MoeSems:

    def __init__(self, sem):
        self.link = sem("link")
        self.var_ready = sem("var_ready")
        self.rstd_ready = sem("rstd_ready")
        self.exp_in = sem("exp_in")
        self.exp_done = sem("exp_done")
        self.routed = sem("routed")
        self.xhat_ready = sem("xhat_ready")
        self.xt_done = sem("xt_done")
        self.ct_done = sem("ct_done")
        self.xh_ready = sem("xh_ready")
        self.g_done = sem("g_done")
        self.silu_done = sem("silu_done")
        self.u_done = sem("u_done")
        self.tu_done = sem("tu_done")
        self.y_out = sem("y_out")
        self.y_turned = sem("y_turned")
        self.hgh_done = sem("hgh_done")
        self.hgl_done = sem("hgl_done")
        self.hg_done = sem("hg_done")
        self.down_done = sem("down_done")
        self.normed = sem("normed")
        self.x_final = sem("x_final")
        self.wo_done = sem("wo_done")
        self.wo_read = sem("wo_read")
        self.xh2_ready = sem("xh2_ready")
        self.xt2_done = sem("xt2_done")
        self.xt2_ready = sem("xt2_ready")
        self.logits_done = sem("logits_done")
        self.logits_ready = sem("logits_ready")
        self.all = [self.link, self.var_ready, self.rstd_ready, self.exp_in, self.exp_done, self.routed,
                    self.xhat_ready, self.xt_done, self.ct_done, self.xh_ready, self.g_done, self.silu_done,
                    self.u_done, self.y_out, self.y_turned, self.hgh_done, self.hgl_done,
                    self.tu_done, self.hg_done, self.down_done, self.normed, self.x_final, self.wo_done,
                    self.wo_read, self.xh2_ready, self.xt2_done, self.xt2_ready, self.logits_done, self.logits_ready]


class Link:

    def __init__(self, engine, sem):
        self.engine, self.sem, self.n = engine, sem, 0

    def __call__(self, instruction):
        self.n += 1
        instruction.then_inc(self.sem, 1)
        self.engine.wait_ge(self.sem, self.n)


class Norms:

    def __init__(self, nc, s, st, mv, ve, rs, half):
        self.nc, self.s, self.st, self.mv, self.ve, self.rs, self.half = nc, s, st, mv, ve, rs, half

    def statistics(self, link, lane, src):
        nc, s = self.nc, self.s
        for t in range(NT):
            last = nc.vector.bn_stats(self.st[:, lane, t, :], src(t))
        link(last)
        for t in range(NT):
            last = nc.vector.bn_aggr(self.mv[:, lane, t, :], self.st[:, lane, t, :])
        link(last)
        nc.vector.tensor_scalar(self.ve[:, lane, :], self.mv[:, lane, :, 1], LN_EPS, None, ALU.add).then_inc(s.var_ready, 1)

    def roots(self, pool, counted, lanes):
        pool.wait_ge(self.s.var_ready, counted)
        n, lanes = len(lanes) * NT, slice(lanes[0], lanes[-1] + 1)
        self.nc.gpsimd.tensor_tensor(self.rs[:, lanes, :].rearrange("p l t -> p (l t)"), self.ve[:, lanes, :].rearrange("p l t -> p (l t)"),
                                     self.half[:, 0:n], ALU.pow).then_inc(self.s.rstd_ready, 1)

    def apply(self, v, lane, n, src, dst, tiles=range(NT)):
        v.wait_ge(self.s.rstd_ready, n)
        for t in tiles:
            last = self.nc.vector.tensor_scalar(dst(t), src(t), self.mv[:, lane, t, 0:1], self.rs[:, lane, t:t + 1], ALU.subtract, ALU.mult)
        return last

    def __call__(self, v, link, n, src, dst, lane=0):
        self.statistics(link, lane, src)
        return self.apply(v, lane, n, src, dst)


def build(nc, x, Wq, Wk, Wv, Wa, ba, Wo, gamma, beta, gate_w, w_gate, w_up, w_down, sw_gate, sw_up, sw_down,
          c_ident, c_masks, c_sel, c_rank, y):
    x_g = x.rearrange("b (u t p) d -> p (b u) t d", t=NT, p=P)
    y_g = y.rearrange("b (u t p) d -> p (b u) t d", t=NT, p=P)
    top = ExitStack()
    with top:
        def sbuf(ctx, name, shape, dt=F32):
            return ctx.enter_context(nc.sbuf_tensor(name, shape, dt))

        def sem(name):
            return top.enter_context(nc.semaphore(name))

        def clear(engine, used):
            for s in used.all:
                engine.sem_clear(s)

        X = sbuf(top, "X", [P, NG * NT, D])
        LG = sbuf(top, "LG", [P, NG * NT, E])
        ident = sbuf(top, "ident", [P, P])
        ST = sbuf(top, "ST", [P, 2, NT, 6])
        MV = sbuf(top, "MV", [P, 2, NT, 2])
        VE = sbuf(top, "VE", [P, 2, NT])
        RS = sbuf(top, "RS", [P, 2, NT])
        HALF = sbuf(top, "HALF", [P, NT * H])
        XHAT = sbuf(top, "XHAT", [P, NT, D])
        XH2 = sbuf(top, "XH2", [P, NT, D])
        OSUM = sbuf(top, "OSUM", [P, NT, D])
        X1 = sbuf(top, "X1", [P, 2, NT, D])
        OT = sbuf(top, "OT", [P, NP_, GT])
        WO = sbuf(top, "WO", [P, NP_, D])
        XT2 = sbuf(top, "XT2", [P, GT])
        GW = sbuf(top, "GW", [P, E])
        GUH = sbuf(top, "GUH", [P, 2, EF + SF], F32R)
        GUR = sbuf(top, "GUR", [P, 2, EF + SF])
        WD = sbuf(top, "WD", [P, NF, D])
        RANK = sbuf(top, "RANK", [P, E])
        CHT = sbuf(top, "CHT", [P, NT, 2 * E])
        CH = sbuf(top, "CH", [P, NT, E], F32R)
        W8 = [sbuf(top, f"W8_{i}", [P, NT, E]) for i in range(4)]
        R1 = [sbuf(top, f"R1_{i}", [P, NT, 1]) for i in range(4)]
        LMAX = sbuf(top, "LMAX", [P, NG * NT, 1])
        XTMP = sbuf(top, "XTMP", [P, GT])
        XH = sbuf(top, "XH", [P, 2, GT], F32R)
        XL = sbuf(top, "XL", [P, 2, GT], F32R)

        load_first, load_rest, load_ffn, stored = sem("load_first"), sem("load_rest"), sem("load_ffn"), sem("stored")
        load_w, load_c, load_sel = sem("load_w"), sem("load_c"), sem("load_sel")

        def group_tile(g, t):
            if isinstance(g, int):
                return X[:, g * NT + t, :]
            return X[:, bass.ds(g * NT + t, 1), :].rearrange("p o d -> p (o d)")

        def group_of(tensor, g):
            return tensor[:, bass.ds(g * NT, NT), :] if not isinstance(g, int) else tensor[:, g * NT:(g + 1) * NT, :]

        def norms(s):
            return Norms(nc, s, ST, MV, VE, RS, HALF)

        def split3(out, wh, wl, xh, xl):
            nc.tensor.matmul(out, wl, xh, start=True, stop=False)
            nc.tensor.matmul(out, wh, xl, start=False, stop=False)
            return nc.tensor.matmul(out, wh, xh, start=False, stop=True)

        def output_product(s, bank):
            for t in range(NT):
                for p in range(NP_):
                    last = nc.tensor.matmul(bank[:, t * P:(t + 1) * P], OT[:, p, t * P:(t + 1) * P], WO[:, p, :],
                                            start=(p == 0), stop=(p == NP_ - 1))
            last.then_inc(s.wo_done, 1)

        def add_residual(v, s, bank, slot):
            v.wait_ge(s.wo_done, 1)
            nc.vector.tensor_tensor(OSUM[:, :, :], bank[:, :].rearrange("p (t d) -> p t d", d=D), X1[:, slot, :, :], ALU.add).then_inc(s.wo_read, 1)
            v.wait_ge(s.wo_read, 1)

        score, work, one, two = (w[:, :, :] for w in W8)
        top1, top2, aux, tot = (r[:, :, :] for r in R1)
        PARTS = 5

        def route(link, part, g, done):
            tt = lambda out, a, b, op: link(nc.vector.tensor_tensor(out, a, b, op))
            most = lambda out, a: link(nc.vector.tensor_reduce(out, a, AX.X, ALU.max))
            wide = lambda r: r.broadcast_to([P, NT, E])
            rank = RANK[:, :].unsqueeze(1).broadcast_to([P, NT, E])

            def candidates(best):
                most(best, score)
                tt(work, score, wide(best), ALU.is_equal)
                tt(work, work, rank, ALU.mult)

            def choose(chosen):
                most(aux, work)
                tt(chosen, work, wide(aux), ALU.is_equal)

            if part == 0:
                link(nc.vector.tensor_reduce(tot, group_of(LG, g), AX.X, ALU.add))
                link(nc.vector.reciprocal(tot, tot))
                tt(score, group_of(LG, g), wide(tot), ALU.mult)
            elif part == 1:
                candidates(top1)
                choose(one)
            elif part == 2:
                link(nc.vector.scalar_tensor_tensor(score, one, -2.0, score, ALU.mult, ALU.add))
                candidates(top2)
            elif part == 3:
                choose(two)
                tt(tot, top1, top2, ALU.add)
                link(nc.vector.tensor_scalar(tot, tot, 1e-20, None, ALU.add))
                link(nc.vector.reciprocal(tot, tot))
            else:
                tt(one, one, wide(top1), ALU.mult)
                tt(two, two, wide(top2), ALU.mult)
                tt(one, one, two, ALU.add)
                link(nc.vector.scalar_tensor_tensor(one, one, SCALE, wide(tot), ALU.mult, ALU.mult))
                link(nc.vector.tensor_copy(CH[:, :, :], one))
                nc.vector.tensor_copy(CHT[:, :, 0:E], CH[:, :, :].bitcast(F32))
                nc.vector.tensor_tensor(CHT[:, :, E:], one, CH[:, :, :].bitcast(F32), ALU.subtract).then_inc(done, 1)

        def centre(link, tiles, done):
            link(nc.vector.tensor_reduce(LMAX[:, tiles, :], LG[:, tiles, :], AX.X, ALU.max))
            n = tiles.stop - tiles.start
            nc.vector.tensor_tensor(LG[:, tiles, :], LG[:, tiles, :], LMAX[:, tiles, :].broadcast_to([P, n, E]), ALU.subtract).then_inc(done, 1)

        BUT_LAST, LAST = slice(0, (NG - 1) * NT), slice((NG - 1) * NT, NG * NT)

        att = ExitStack()
        with att:
            WH = sbuf(att, "WH", [P, 4, H * DH], F32R)
            WL = sbuf(att, "WL", [P, 4, H * DH], F32R)
            BA = sbuf(att, "BA", [P, NP_])
            GB = sbuf(att, "GB", [P, 2])
            MASK = sbuf(att, "MASK", [P, 4, P], U32)
            X1N = sbuf(att, "X1N", [P, NT, D])
            Q0 = sbuf(att, "Q0", [P, 2, 2, GT])
            Q = sbuf(att, "Q", [P, NP_, 2, GT])
            K = sbuf(att, "K", [P, NP_, GT])
            KSQ = sbuf(att, "KSQ", [P, GT])
            KT = sbuf(att, "KT", [P, 2, GT])
            DG = sbuf(att, "DG", [P, NT, H])
            N2 = sbuf(att, "N2", [P, NT, H])
            RN = sbuf(att, "RN", [P, NT, H])
            AL = sbuf(att, "AL", [P, NP_, GT])
            TT = sbuf(att, "TT", [P, NP_, GT])
            V = sbuf(att, "V", [P, NT, H * DH])
            AT = sbuf(att, "AT", [P, 2, NT * 2, P])
            KTOK = sbuf(att, "KTOK", [P, 2, NT, P])
            S = sbuf(att, "S", [P, NP_, NT + 1, P])
            QK = OSUM[:, :, :].rearrange("p t d -> p (t d)")
            RAW = Q[:, :, 0, :]
            L = [att.enter_context(nc.psum_tensor(f"L{i}", [P, 2 * NT * P], F32)) for i in range(2)]
            PJ = [att.enter_context(nc.psum_tensor(f"PJ{i}", [P, GT], F32)) for i in range(2)]
            OB = [att.enter_context(nc.psum_tensor(f"OB{i}", [P, GT], F32)) for i in range(2)]

            def take_input(act, s, got, slot):
                nc.scalar.activation(XTMP[:, :], got, ACT.Identity, scale=GB[:, 0:1], bias=GB[:, 1:2]).then_inc(s.xn_tmp, 1)
                act.wait_ge(s.xn_tmp, 1)
                nc.scalar.activation(XH[:, slot, :], XTMP[:, :], ACT.Copy).then_inc(s.xh_ready, 1)

            def input_remainder(pool, s, slot):
                pool.wait_ge(s.xh_ready, 1)
                nc.gpsimd.tensor_tensor(XL[:, slot, :], XTMP[:, :], XH[:, slot, :].bitcast(F32), ALU.subtract).then_inc(s.xl_ready, 1)

            A = [AttentionSems(lambda name: sem(f"a{i}_{name}")) for i in range(2)]

            with nc.Block() as block:
                s = A[0]

                @block.sync
                def _(sp):
                    sp.dma_start(X[:, 0:NT, :], x_g[:, 0, :, :]).then_inc(load_first, 16)
                    for i, w in enumerate((Wq, Wk, Wv, Wa)):
                        sp.dma_start(RAW[:, i, :], w).then_inc(load_w, 16)
                    sp.dma_start(ident[:, :], c_ident).then_inc(load_c, 16)
                    with nc.allow_non_contiguous_dma(reason="small vectors put on partitions"):
                        sp.dma_start(BA[:, :], ba.rearrange("(n p) -> p n", p=P)).then_inc(load_c, 16)
                        sp.dma_start(GB[:, 0:1], gamma.rearrange("(p o) -> p o", o=1)).then_inc(load_c, 16)
                        sp.dma_start(GB[:, 1:2], beta.rearrange("(p o) -> p o", o=1)).then_inc(load_c, 16)
                        sp.dma_start(GW[:, :], gate_w.rearrange("e d -> d e")).then_inc(load_c, 16)
                    sp.dma_start(MASK[:, :, :], c_masks).then_inc(load_c, 16)
                    sp.dma_start(WO[:, :, :], Wo.rearrange("(n p) d -> p n d", p=P)).then_inc(load_c, 16)
                    sp.dma_start(X[:, NT:, :].rearrange("p (g t) d -> p g t d", t=NT), x_g[:, 1:, :, :]).then_inc(load_rest, 16)
                    for i, (we, ws) in enumerate(((w_gate, sw_gate), (w_up, sw_up))):
                        sp.dma_start(GUR[:, i, 0:EF].rearrange("p (e f) -> p e f", f=F), we.rearrange("e d f -> d e f")).then_inc(load_ffn, 16)
                        sp.dma_start(GUR[:, i, EF:], ws).then_inc(load_ffn, 16)
                    sp.dma_start(RANK[:, :], c_rank).then_inc(load_ffn, 16)
                    sp.dma_start(WD[:, 0:FT, :], w_down.rearrange("e f d -> (e f) d").rearrange("(t p) d -> p t d", p=P)).then_inc(load_ffn, 16)
                    sp.dma_start(WD[:, FT:FT + 2, :], sw_down[0:2 * P, :].rearrange("(t p) d -> p t d", p=P)).then_inc(load_ffn, 16)
                    sp.dma_start(WD[0:SF - 2 * P, FT + 2, :], sw_down[2 * P:SF, :]).then_inc(load_ffn, 16)
                    sp.wait_ge(load_c, 7 * 16)

                @block.gpsimd
                def _(pool):
                    nc.gpsimd.memset(HALF[:, :], -0.5).then_inc(s.q_one, 1)
                    nc.gpsimd.memset(Q0[:, :, :, :], 0.0)
                    pool.wait_ge(s.q_one, 1)
                    norm = norms(s)
                    norm.roots(pool, 1, [0])
                    norm.roots(pool, 2, [0])
                    pool.wait_ge(s.act_evac, 1)
                    nc.gpsimd.tensor_tensor(WL[:, 0:2, :], RAW[:, 0:2, :], WH[:, 0:2, :].bitcast(F32), ALU.subtract)
                    input_remainder(pool, s, 0)

                @block.scalar
                def _(act):
                    act.wait_ge(load_w, 4 * 16)
                    nc.scalar.activation(WH[:, :, :], RAW, ACT.Copy).then_inc(s.act_evac, 1)
                    act.wait_ge(s.xt_done, 1)
                    take_input(act, s, OB[1][:, :], 0)

                @block.tensor
                def _(pe):
                    pe.wait_ge(load_c, 7 * 16)
                    pe.wait_ge(s.xhat_ready, 1)
                    for t in range(NT):
                        last = nc.tensor.transpose(OB[1][:, t * P:(t + 1) * P], XHAT[:, t, :], ident[:, :])
                    last.then_inc(s.xt_done, 1)

                @block.vector
                def _(v):
                    link, norm = Link(v, s.link), norms(s)
                    v.wait_ge(load_first, 16)
                    x1 = lambda t: X1[:, 0, t, :]
                    link(norm(v, link, 1, lambda t: group_tile(0, t), x1))
                    norm(v, link, 2, x1, lambda t: XHAT[:, t, :]).then_inc(s.xhat_ready, 1)
                    v.wait_ge(s.act_evac, 1)
                    nc.vector.tensor_tensor(WL[:, 2:4, :], RAW[:, 2:4, :], WH[:, 2:4, :].bitcast(F32), ALU.subtract)

            FIRST = [[], [("k", 2), ("q", 2)], [("a", 2), ("k", 3)], [("q", 3)], [("a", 3)], [("v", 0), ("v", 1)], [("v", 2), ("v", 3)], []]
            BETWEEN = [("r", 0), ("r", 1), ("t", 0)]
            SECOND = [[], [], [("k", 4)], [("x", 0), ("q", 4)], [("l", 0), ("a", 4)], [("k", 5), ("q", 5)], [("a", 5), ("n", 0), ("m", 0)], [("n", 1), ("m", 1)]]
            END = [("n", 2), ("m", 2), ("n", 3), ("r", 2), ("m", 3), ("r", 3)]
            NEXT = [it for it in sum(SECOND, []) + END if it[0] in "kqanm"]
            NL = len(LEVELS)

            def attention_block(g, hf, start=False, first=False, final=False):
                s, other = A[hf], A[1 - hf]
                left_out = lambda it: first and it[0] in "xl" or final and (it in NEXT or it[0] == "t") or start and it not in NEXT
                items = [it for it in sum(FIRST, []) + BETWEEN + sum(SECOND, []) + END if not left_out(it)]
                at_item = {it: i for i, it in enumerate(items)}
                taker = lambda i: {"v": s.v_scaled, "m": s.qt_read}.get(items[i][0], s.act_evac)
                taken = [sum(1 for j in range(i + 1) if taker(j) is taker(i)) for i in range(len(items))]
                evac = lambda *item: taken[at_item[item]]
                lv = lambda c, l, i: (c * (NL - 1) + l - 1) * 2 + i + 1
                up = lambda c, l, i: (c * (NL - 1) + l - 1) * 2 + i + 1
                uq = lambda c, l, i: (c * (NL - 3) + l - 2) * 2 + i + 1
                mg = lambda c, l, i: (c * (BLOCKS - 1) + l - 1) * 2 + i + 1
                pl = lambda c, l, i: (c * (NL - BLOCKS) + l - BLOCKS) * 2 + i + 1

                with nc.Block() as block:
                    @block.sync
                    def _(sp):
                        clear(sp, other)

                    @block.tensor
                    def _(pe):
                        def item(kind, n):
                            if (kind, n) not in at_item:
                                return
                            i = at_item[kind, n]
                            bank = PJ[i % 2]
                            if i >= 2:
                                pe.wait_ge(taker(i - 2), taken[i - 2])
                            x = 1 - hf if kind in "nm" or kind in "kqa" and n >= NP_ else hf
                            if x != hf and not start:
                                pe.wait_ge(s.xl_ready, 1)
                            if kind in "kqa":
                                w, p = "qkva".index(kind), n % NP_
                                cols = slice(p * P, (p + 1) * P)
                                last = split3(bank[:, :], WH[:, w, cols], WL[:, w, cols], XH[:, x, :], XL[:, x, :])
                            elif kind in "mnv":
                                w, toks = "qkva".index({"m": "q", "n": "k", "v": "v"}[kind]), slice(n * P, (n + 1) * P)
                                last = split3(bank[:, :], XH[:, x, toks], XL[:, x, toks], WH[:, w, :], WL[:, w, :])
                            elif kind in "xt":
                                ready, src = (s.xh2_ready, XH2) if kind == "x" else (s.xhat_ready, XHAT)
                                pe.wait_ge(ready, 1)
                                for t in range(NT):
                                    last = nc.tensor.transpose(bank[:, t * P:(t + 1) * P], src[:, t, :], ident[:, :])
                            elif kind == "l":
                                pe.wait_ge(s.act_evac, evac("x", 0))
                                for t in range(NT):
                                    last = nc.tensor.matmul(bank[:, t * E:(t + 1) * E], XT2[:, t * P:(t + 1) * P], GW[:, :],
                                                            start=True, stop=True)
                            else:
                                pe.wait_ge(s.k_up, up(n // 2, NL - 1, n % 2))
                                for t in range(NT):
                                    last = nc.tensor.transpose(bank[:, t * P:(t + 1) * P], K[:, n, t * P:(t + 1) * P], ident[:, :])
                            last.then_inc(s.proj_done, 1)

                        def level(c, l, i):
                            p, sz = 2 * c + i, LEVELS[l]
                            if l == 1:
                                if c:
                                    pe.wait_ge(s.s_step, NT * (i + 1))
                                    pe.wait_ge(s.q_one, i + 1)
                            else:
                                if l == 2:
                                    pe.wait_ge(s.q_two, 2 * c + i + 1)
                                else:
                                    pe.wait_ge(s.q_up, uq(c, l - 1, i))
                                pe.wait_ge(s.k_up, up(c, l - 1, i))
                                if 2 < l < BLOCKS + 2:
                                    pe.wait_ge(s.merged, mg(c, l - 2, i))
                                elif l >= BLOCKS + 2:
                                    pe.wait_ge(s.placed, pl(c, l - 2, i))
                            for t in range(NT):
                                k = K[:, p, t * P:(t + 1) * P]
                                q = Q[:, p, :, t * P:(t + 1) * P]
                                at = BANK[l] * GT
                                if l < BLOCKS:
                                    last = nc.tensor.matmul(L[i][:, at + t * P:at + (t + 1) * P], k,
                                                            q.rearrange("p h (m two s) -> p h m two s", two=2, s=sz)[:, :, :, 1, :],
                                                            start=True, stop=True)
                                    continue
                                for b in range(0, P, 2 * sz):
                                    last = nc.tensor.matmul(L[i][b:b + sz, at + 2 * t * sz:at + 2 * (t + 1) * sz], k[:, b:b + sz],
                                                            q[:, :, b + sz:b + 2 * sz], start=True, stop=True)
                            last.then_inc(s.lv_done, 1)

                        def both(c, l, its):
                            between = 1 if l >= BLOCKS and len(its) > 1 else 0
                            if l:
                                level(c, l, 0)
                            for it in its[:between]:
                                item(*it)
                            if l:
                                level(c, l, 1)
                            if (c, l) == (0, 1) and not first:
                                pe.wait_ge(s.ot_last, 1)
                                output_product(s, OB[0])
                            for it in its[between:]:
                                item(*it)

                        def within_tiles(c, i):
                            p = 2 * c + i
                            pe.wait_ge(s.merged, mg(c, BLOCKS - 1, i))
                            pe.wait_ge(s.placed, pl(c, NL - 1, i))
                            pe.wait_ge(s.v_scaled, NT)
                            if c:
                                pe.wait_ge(s.ot_ready, i + 1)
                            elif i == 0 and not first:
                                pe.wait_ge(s.wo_read, 1)
                            for t in range(NT):
                                for h in range(2):
                                    last = nc.tensor.matmul(OB[i][h * DH:(h + 1) * DH, t * P:(t + 1) * P],
                                                            V[:, t, (2 * p + h) * DH:(2 * p + h + 1) * DH],
                                                            AT[:, i, 2 * t + h, :], start=(t == 0),
                                                            stop=(hf == 0 and t == 0), skip_group_check=True)
                            last.then_inc(s.within_done, 1)

                        def key_values(c, i):
                            p = 2 * c + i
                            pe.wait_ge(s.act_evac, evac("r", p))
                            for t in range(NT):
                                last = nc.tensor.matmul(L[i][:, t * P:(t + 1) * P], KTOK[:, i, t, :],
                                                        V[:, t, p * P:(p + 1) * P], start=True, stop=True)
                            last.then_inc(s.kv_done, 1)

                        def from_states(c, i):
                            p = 2 * c + i
                            pe.wait_ge(s.q_last, p + 1)
                            for t in range(1 if hf == 0 else 0, NT):
                                if t:
                                    pe.wait_ge(s.s_step, p * NT + t)
                                else:
                                    pe.wait_ge(s.carried, 1)
                                for h in range(2):
                                    last = nc.tensor.matmul(OB[i][h * DH:(h + 1) * DH, t * P:(t + 1) * P],
                                                            S[:, p, t, h * DH:(h + 1) * DH], Q[:, p, h, t * P:(t + 1) * P],
                                                            start=False, stop=True, skip_group_check=True)
                            last.then_inc(s.o_done, 1)

                        if start:
                            for it in items:
                                item(*it)
                            return
                        for l in range(NL):
                            both(0, l, FIRST[l])
                        for it in BETWEEN[:2]:
                            item(*it)
                        for i in range(2):
                            within_tiles(0, i)
                            key_values(0, i)
                        item(*BETWEEN[2])
                        for l in range(NL):
                            both(1, l, SECOND[l])
                            if l < 2:
                                from_states(0, l)
                        item("n", 2)
                        within_tiles(1, 0)
                        item("m", 2)
                        item("n", 3)
                        within_tiles(1, 1)
                        for it in END[3:]:
                            item(*it)
                        for i in range(2):
                            key_values(1, i)
                        for i in range(2):
                            from_states(1, i)

                    @block.scalar
                    def _(act):
                        def item(kind, n):
                            if kind in "mv" or (kind, n) not in at_item:
                                return
                            i = at_item[kind, n]
                            act.wait_ge(s.proj_done, i + 1)
                            bank = PJ[i % 2]
                            if kind == "k":
                                last = nc.scalar.activation(K[:, n % NP_, :], bank[:, :], ACT.Copy)
                            elif kind == "n":
                                if n >= 2:
                                    act.wait_ge(s.qt_read, n - 1)
                                nc.scalar.activation(KT[:, n % 2, :], bank[:, :], ACT.Copy)
                                if n:
                                    act.wait_ge(s.sq_read, n)
                                last = nc.scalar.activation(KSQ[:, :], bank[:, :], ACT.Square)
                            elif kind == "q":
                                if n >= NP_ and not start:
                                    act.wait_ge(s.q_one, n - NP_ + 1)
                                for h in range(2):
                                    rows = slice(h * DH, (h + 1) * DH)
                                    last = nc.scalar.activation(Q0[rows, n % 2, h, :], bank[rows, :], ACT.Copy)
                            elif kind == "a":
                                p = n % NP_
                                last = nc.scalar.activation(AL[:, p, :], bank[:, :], ACT.Sigmoid, bias=BA[:, p:p + 1])
                            elif kind == "t":
                                take_input(act, s, bank[:, :], 1 - hf)
                                act.sem_inc(s.act_evac, 1)
                                return
                            elif kind == "x":
                                last = nc.scalar.activation(XT2[:, :], bank[:, :], ACT.Copy)
                            elif kind == "l":
                                last = nc.scalar.activation(group_of(LG, g - 1), bank[:, 0:NT * E].rearrange("p (t e) -> p t e", e=E), ACT.Copy)
                            else:
                                last = nc.scalar.activation(KTOK[:, n % 2, :, :].rearrange("p t k -> p (t k)"), bank[:, :], ACT.Copy)
                            last.then_inc(s.act_evac, 1)

                        def place(c, l, i):
                            sz = LEVELS[l]
                            act.wait_ge(s.lv_done, lv(c, l, i))
                            act.wait_ge(s.merged, mg(c, BLOCKS - 1, i))
                            for b in range(0, P, 2 * sz):
                                at = BANK[l] * GT
                                last = nc.scalar.activation(AT[b:b + sz, i, :, b + sz:b + 2 * sz],
                                                            L[i][b:b + sz, at:at + 2 * NT * sz].rearrange("p (n i) -> p n i", i=sz), ACT.Copy)
                            last.then_inc(s.placed, 1)

                        def both(c, l, its):
                            between = 1 if l >= BLOCKS and len(its) > 1 else 0
                            if l >= BLOCKS:
                                place(c, l, 0)
                            for it in its[:between]:
                                item(*it)
                            if l >= BLOCKS:
                                place(c, l, 1)
                            for it in its[between:]:
                                item(*it)

                        def take_outputs(c, i):
                            act.wait_ge(s.o_done, 2 * c + i + 1)
                            nc.scalar.activation(OT[:, 2 * c + i, :], OB[i][:, :], ACT.Copy).then_inc(s.ot_ready, 1)

                        def last_update(c, i):
                            p = 2 * c + i
                            act.wait_ge(s.lv_done, lv(c, NL - 1, i))
                            for t in range(NT):
                                q = Q[:, p, :, t * P + DH:(t + 1) * P]
                                last = nc.scalar.activation(q, q, ACT.Copy, scale=run_products(p, DH)[:, t, 0:1])
                            last.then_inc(s.q_last, 1)

                        if start:
                            for it in items:
                                item(*it)
                            return
                        if not first:
                            nc.scalar.activation(OT[:, NP_ - 1, :], OB[1][:, :], ACT.Copy).then_inc(s.ot_last, 1)
                        for i in range(2):
                            for n in range(2 * NT):
                                h = 2 * i + n % 2
                                last = nc.scalar.activation(AT[:, i, n, :], ident[:, :], ACT.Copy, scale=DG[:, n // 2, h:h + 1])
                            last.then_inc(s.based_act, 1)
                        for l in range(NL):
                            if l == 2 and not final:
                                act.wait_ge(s.x1_ready, 1)
                                if not first:
                                    act.wait_ge(s.wo_read, 1)
                                nc.scalar.activation(X1[:, 1 - hf, :, :], X1N[:, :, :], ACT.Copy)
                            both(0, l, FIRST[l])
                        for it in BETWEEN[:2]:
                            item(*it)
                        for i in range(2):
                            last_update(0, i)
                        item(*BETWEEN[2])
                        for l in range(NL):
                            both(1, l, SECOND[l])
                            if final and l == 5:
                                act.wait_ge(s.exp_in, 1)
                                nc.scalar.activation(LG[:, BUT_LAST, :], LG[:, BUT_LAST, :], ACT.Exp).then_inc(s.exp_done, 1)
                            if l < 2:
                                take_outputs(0, l)
                                if final:
                                    act.wait_ge(load_ffn, 8 * 16)
                                    nc.scalar.activation(GUH[:, l, :], GUR[:, l, :], ACT.Copy)
                        for i in range(2):
                            item("n", 2 + i)
                            last_update(1, i)
                        for i in range(2):
                            item("r", 2 + i)
                        for i in range(2 if final else 1):
                            take_outputs(1, i)

                    @block.gpsimd
                    def _(pool):
                        def first_runs(p):
                            pool.wait_ge(s.act_evac, evac("a", p))
                            if p >= NP_ and not start:
                                pool.wait_ge(s.o_done, p - NP_ + 1)
                            one_run(nc.gpsimd, p).then_inc(s.q_one, 1)

                        def gate_products(c):
                            pair = slice(2 * c % NP_, 2 * c % NP_ + 2)
                            before = 7 if c == 2 and not start else 0
                            pool.wait_ge(s.act_evac, evac("a", 2 * c + 1))
                            if before:
                                pool.wait_ge(s.s_step, 2 * NT)
                            for n, sz in enumerate((2, 4, 8, 16, 32, 64, 128)):
                                src = AL[:, pair, :] if sz == 2 else TT[:, pair, T_AT[sz // 2]:T_AT[sz // 2] + 2 * GT // sz]
                                src = src.rearrange("p n (m two) -> p n m two", two=2)
                                if n:
                                    pool.wait_ge(s.t_ready, before + n)
                                nc.gpsimd.tensor_tensor(TT[:, pair, T_AT[sz]:T_AT[sz] + GT // sz], src[:, :, :, 0],
                                                        src[:, :, :, 1], ALU.mult).then_inc(s.t_ready, 1)

                        def update(c, l, i):
                            pool.wait_ge(s.lv_done, lv(c, l, i))
                            if c:
                                pool.wait_ge(s.t_ready, l - 1)
                            q_update(nc.gpsimd, 2 * c + i, LEVELS[l]).then_inc(s.q_up, 1)

                        def key_norms(t):
                            nc.gpsimd.tensor_tensor(RN[:, t, :], N2[:, t, :], HALF[:, 0:H], ALU.pow).then_inc(s.rn_ready, 1)

                        def prepare_next():
                            for p in (NP_,) if start else (NP_, NP_ + 1):
                                first_runs(p)
                            gate_products(2)

                        if start:
                            prepare_next()
                            return
                        norm = norms(s)
                        key_norms(0)
                        norm.roots(pool, 1, [1])
                        for t in range(1, NT):
                            key_norms(t)
                        for l in range(2, NL - 1):
                            for i in range(2):
                                update(0, l, i)
                            if l == 2:
                                norm.roots(pool, 2 if first or final else 3, ([] if first else [0]) + ([] if final else [1]))
                        first_runs(2)
                        first_runs(3)
                        if not first:
                            norm.roots(pool, 3 if final else 4, [0])
                        gate_products(1)
                        if not final:
                            input_remainder(pool, s, 1 - hf)
                        for l in range(2, NL - 1):
                            for i in range(2):
                                update(1, l, i)
                        if not final:
                            prepare_next()

                    @block.vector
                    def _(v):
                        link, norm = Link(v, s.link), norms(s)

                        def own_keys(tiles):
                            for t in tiles:
                                v.wait_ge(s.act_evac, evac("n", t))
                                heads = lambda ap: ap.rearrange("p (h d) -> p h d", d=DH)
                                nc.vector.tensor_reduce(N2[:, t, :], heads(KSQ[:, :]), AX.X, ALU.add).then_inc(s.sq_read, 1)
                                i = at_item["m", t]
                                v.wait_ge(s.proj_done, i + 1)
                                nc.vector.tensor_tensor(QK, PJ[i % 2][:, :], KT[:, t % 2, :], ALU.mult).then_inc(s.qt_read, 1)
                                v.wait_ge(s.qt_read, t + 1)
                                link(nc.vector.tensor_reduce(DG[:, t, :], heads(QK), AX.X, ALU.add))
                                nc.vector.tensor_scalar(N2[:, t, :], N2[:, t, :], NORM_EPS ** 2, None, ALU.max)

                        def scale_values(t):
                            v.wait_ge(s.rn_ready, t + 1)
                            i = at_item["v", t]
                            v.wait_ge(s.proj_done, i + 1)
                            nc.vector.tensor_tensor(V[:, t, :].rearrange("p (h d) -> p h d", d=DH),
                                                    PJ[i % 2][:, :].rearrange("p (h d) -> p h d", d=DH),
                                                    RN[:, t, :].unsqueeze(2).broadcast_to([P, H, DH]), ALU.mult).then_inc(s.v_scaled, 1)

                        x2, xh2 = lambda t: group_tile(g - 1, t), lambda t: XH2[:, t, :]
                        attended = lambda t: OSUM[:, t, :]
                        coming, x1 = lambda t: group_tile(0 if final else g + 1, t), lambda t: X1N[:, t, :]


                        def beside(l):
                            if final:
                                if l == 1:
                                    norm.apply(v, 1, 1, coming, lambda t: XHAT[:, t, :])
                            if not first:
                                if l == 1:
                                    add_residual(v, s, OB[0], 1 - hf)
                                    norm.statistics(link, 0, attended)
                                elif l == 4:
                                    link(norm.apply(v, 0, 2, attended, attended))
                                elif l == 6:
                                    link(nc.vector.tensor_tensor(group_of(X, g - 1), group_of(X, g - 1), OSUM[:, :, :], ALU.add))
                                elif l == 7:
                                    norm.statistics(link, 0, x2)

                        def diagonal(i):
                            p = 2 + i
                            v.wait_ge(s.within_done, i + 1)
                            nc.vector.tensor_tensor(AT[:, i, :, :].rearrange("p (t h) i -> p t h i", h=2),
                                                    ident[:, :].unsqueeze(1).unsqueeze(1).broadcast_to([P, NT, 2, P]),
                                                    DG[:, :, 2 * p:2 * p + 2].unsqueeze(3).broadcast_to([P, NT, 2, P]), ALU.mult).then_inc(s.based, 1)

                        def k_update(c, l, i):
                            p, sz = 2 * c + i, LEVELS[l]
                            v.wait_ge(s.lv_done, lv(c, l, i))
                            if c and sz > 1:
                                v.wait_ge(s.t_ready, l - 1)
                            k = K[:, p, :].rearrange("p (m two s) -> p m two s", two=2, s=sz)[:, :, 0, :]
                            t = run_products(p, sz)[:, :, 1].unsqueeze(2).broadcast_to([P, GT // sz // 2, sz])
                            nc.vector.tensor_tensor(k, k, t, ALU.mult).then_inc(s.k_up, 1)

                        def merge(c, l, i):
                            sz = LEVELS[l]
                            m = P // sz // 2
                            seconds = lambda ap: ap.rearrange("p n (m two s) -> p n m two s", two=2, s=sz)[:, :, :, 1, :]
                            got = L[i][:, BANK[l] * GT:(BANK[l] + 1) * GT].rearrange("p (n m s) -> p n m s", m=m, s=sz)
                            mask = seconds(MASK[:, l - 1, :].unsqueeze(1)).broadcast_to([P, 2 * NT, m, sz])
                            if l == 1:
                                v.wait_ge(s.based if c else s.based_act, i + 1)
                            else:
                                v.wait_ge(s.merged, mg(c, l - 1, i))
                            nc.vector.copy_predicated(seconds(AT[:, i, :, :]), mask, got).then_inc(s.merged, 1)

                        def levels(c):
                            for l in range(1, NL):
                                if l == 1:
                                    for i in range(2):
                                        k_update(c, 1, i)
                                        q_update(nc.vector, 2 * c + i, 1).then_inc(s.q_two, 1)
                                    merge(c, 1, 0)
                                    if c == 0 and not final:
                                        norm.apply(v, 1, 1, coming, x1).then_inc(s.x1_ready, 1)
                                        v.wait_ge(s.x1_ready, 1)
                                        norm.statistics(link, 1, x1)
                                    merge(c, 1, 1)
                                else:
                                    for i in range(2):
                                        k_update(c, l, i)
                                        if c == 0 and len(FIRST[l]) > i and FIRST[l][i][0] == "v":
                                            scale_values(FIRST[l][i][1])
                                        if l < BLOCKS:
                                            merge(c, l, i)
                                if c == 0:
                                    beside(l)
                                elif l == 1 and not first:
                                    norm.apply(v, 0, 3, x2, xh2, range(0, NT // 2))
                                elif l == 2 and not first:
                                    norm.apply(v, 0, 3, x2, xh2, range(NT // 2, NT)).then_inc(s.xh2_ready, 1)
                                elif l == 6 and not final:
                                    own_keys([0])
                                elif final and l == 4:
                                    v.wait_ge(s.act_evac, evac("l", 0))
                                    centre(link, BUT_LAST, s.exp_in)
                                elif final and l > 4:
                                    if l == 5:
                                        v.wait_ge(s.exp_done, 1)
                                        v.wait_ge(load_ffn, 8 * 16)
                                    route(link, l - 5, 0, s.routed)

                        def states(c):
                            for i in range(2):
                                p = 2 * c + i
                                v.wait_ge(s.kv_done, p + 1)
                                for t in range(NT):
                                    kv = L[i][:, t * P:(t + 1) * P]
                                    if t:
                                        v.wait_ge(s.s_step, p * NT + t)
                                    if t == 0 and hf == 0:
                                        ins = nc.vector.tensor_copy(S[:, p, 1, :], kv)
                                    else:
                                        ins = nc.vector.scalar_tensor_tensor(S[:, p, t + 1, :], S[:, p, t, :],
                                                                             TT[:, p, T_AT[128] + t:T_AT[128] + t + 1], kv, ALU.mult, ALU.add)
                                    ins.then_inc(s.s_step, 1)

                        if start:
                            v.wait_ge(s.act_evac, evac("a", NP_ + 1))
                            one_run(nc.vector, NP_ + 1)
                            own_keys(range(NT))
                            return
                        if hf:
                            nc.vector.tensor_copy(S[:, :, 0, :], S[:, :, NT, :]).then_inc(s.carried, 1)
                            v.wait_ge(s.carried, 1)
                        if first:
                            v.wait_ge(load_rest, 16)
                        norm.statistics(link, 1, coming)
                        levels(0)
                        if not final:
                            norm.apply(v, 1, 2, x1, lambda t: XHAT[:, t, :]).then_inc(s.xhat_ready, 1)
                        for i in range(2):
                            diagonal(i)
                        states(0)
                        levels(1)
                        if not final:
                            own_keys(range(1, NT))
                        if final:
                            for part in range(NL - 5, PARTS):
                                route(link, part, 0, s.routed)
                        states(1)

            def q_update(engine, p, sz):
                q = Q[:, p, :, :].rearrange("p h (m two s) -> p h m two s", two=2, s=sz)[:, :, :, 1, :]
                t = run_products(p, sz)[:, :, 0].unsqueeze(1).unsqueeze(3).broadcast_to([P, 2, GT // sz // 2, sz])
                return engine.tensor_tensor(q, q, t, ALU.mult)

            def one_run(engine, p):
                return engine.tensor_tensor(Q[:, p % NP_, :, :], Q0[:, p % 2, :, :],
                                            AL[:, p % NP_, :].unsqueeze(1).broadcast_to([P, 2, GT]), ALU.mult)

            def run_products(p, sz):
                src = AL[:, p, :] if sz == 1 else TT[:, p, T_AT[sz]:T_AT[sz] + GT // sz]
                return src.rearrange("p (m two) -> p m two", two=2)

            attention_block(-1, 1, start=True)
            attention_block(0, 0, first=True)
            with nc.Fori(0, NG // 2 - 1) as b:
                attention_block(b * 2 + 1, 1)
                attention_block(b * 2 + 2, 0)
            attention_block(NG - 1, 1, final=True)

        moe = ExitStack()
        with moe:
            GUL = sbuf(moe, "GUL", [P, 2, EF + SF], F32R)
            SELR = sbuf(moe, "SELR", [2 * E, FT, P])
            SEL = sbuf(moe, "SEL", [2 * E, FT, P], F32R)
            CT = sbuf(moe, "CT", [2 * E, 2, GT], F32R)
            SG = sbuf(moe, "SG", [P, 2, GT])
            TU = sbuf(moe, "TU", [P, 2, GT])
            HG = sbuf(moe, "HG", [P, LAG + 1, GT])
            HGH = sbuf(moe, "HGH", [P, LAG + 1, GT], F32R)
            HGL = sbuf(moe, "HGL", [P, LAG + 1, GT], F32R)
            WDH = sbuf(moe, "WDH", [P, SPLIT, D], F32R)
            WDL = sbuf(moe, "WDL", [P, SPLIT, D], F32R)
            YS = sbuf(moe, "YS", [P, GT])
            G = [moe.enter_context(nc.psum_tensor(f"G{i}", [P, GT], F32)) for i in range(2)]
            U = [moe.enter_context(nc.psum_tensor(f"U{i}", [P, GT], F32)) for i in range(2)]
            C = [moe.enter_context(nc.psum_tensor(f"C{i}", [P, GT], F32)) for i in range(2)]
            Y = [moe.enter_context(nc.psum_tensor(f"Y{i}", [P, GT], F32)) for i in range(2)]
            M = [MoeSems(lambda name: sem(f"m{i}_{name}")) for i in range(2)]

            def transpose_input():
                for t in range(NT):
                    last = nc.tensor.transpose(C[0][:, t * P:(t + 1) * P], XHAT[:, t, :], ident[:, :])
                return last

            def transpose_routing():
                for t in range(NT):
                    last = nc.tensor.transpose(C[1][0:2 * E, t * P:(t + 1) * P], CHT[:, t, :], ident[:, :])
                return last

            def take_coming(act, s, slot):
                act.wait_ge(s.xt_done, 1)
                nc.scalar.activation(XH[:, slot, :], C[0][:, :], ACT.Copy).then_inc(s.xh_ready, 1)

            def take_routing(act, s, slot):
                act.wait_ge(s.ct_done, 1)
                nc.scalar.activation(CT[:, slot, :], C[1][0:2 * E, :], ACT.Copy)

            def coming_remainder(v, s, slot):
                v.wait_ge(s.xh_ready, 1)
                nc.vector.tensor_tensor(XL[:, slot, :], C[0][:, :], XH[:, slot, :].bitcast(F32), ALU.subtract)

            with nc.Block() as block:
                s = M[0]

                @block.sync
                def _(sp):
                    sp.dma_start(SELR[:, :, :], c_sel).then_inc(load_sel, 16)

                @block.tensor
                def _(pe):
                    transpose_input().then_inc(s.xt_done, 1)
                    transpose_routing().then_inc(s.ct_done, 1)

                @block.scalar
                def _(act):
                    take_coming(act, s, 0)
                    take_routing(act, s, 0)
                    act.wait_ge(load_sel, 16)
                    nc.scalar.activation(SEL[:, :, :], SELR[:, :, :], ACT.Copy)

                @block.gpsimd
                def _(pool):
                    nc.gpsimd.tensor_tensor(GUL[:, 0, :], GUR[:, 0, :], GUH[:, 0, :].bitcast(F32), ALU.subtract)

                @block.vector
                def _(v):
                    nc.vector.tensor_tensor(GUL[:, 1, :], GUR[:, 1, :], GUH[:, 1, :].bitcast(F32), ALU.subtract)
                    coming_remainder(v, s, 0)
                    nc.vector.tensor_copy(WDH[:, :, :], WD[:, 0:SPLIT, :])

            def store(sp, s, g):
                sp.wait_ge(s.x_final, 1)
                if isinstance(g, int):
                    sp.dma_start(y_g[:, g - 1, :, :], X[:, (g - 1) * NT:g * NT, :]).then_inc(stored, 16)
                else:
                    sp.dma_start(y_g[:, bass.ds(g - 1, 1), :, :].rearrange("p o t d -> p (o t) d"),
                                 X[:, bass.ds((g - 1) * NT, NT), :]).then_inc(stored, 16)

            def moe_block(g, hf, first=False, final=False):
                s, other = M[1 - hf], M[hf]
                spare = Y[1 - hf]
                with nc.Block() as block:
                    @block.sync
                    def _(sp):
                        clear(sp, other)
                        if not first:
                            store(sp, s, g)

                    @block.tensor
                    def _(pe):
                        def hidden(f):
                            col, rows = f * P, FTILES[f][1]
                            cols = slice(col, col + rows)
                            if f >= 2:
                                pe.wait_ge(s.silu_done, f - 1)
                            split3(G[f % 2][0:rows, :], GUH[:, 0, cols], GUL[:, 0, cols], XH[:, hf, :], XL[:, hf, :]).then_inc(s.g_done, 1)
                            if f >= 2:
                                pe.wait_ge(s.tu_done, f - 1)
                            last = split3(U[f % 2][0:rows, :], GUH[:, 1, cols], GUL[:, 1, cols], XH[:, hf, :], XL[:, hf, :])
                            if f < FT:
                                if f >= 2:
                                    pe.wait_ge(s.hg_done, f - 1)
                                last = nc.tensor.matmul(C[f % 2][:, :], SEL[:, f, :], CT[:, hf, :], start=True, stop=True)
                            last.then_inc(s.u_done, 1)

                        def down(f):
                            rows = FTILES[f][1]
                            out = Y[hf][:, :]
                            if f >= SPLIT:
                                pe.wait_ge(s.hg_done, f + 1)
                                nc.tensor.matmul(out, WD[0:rows, f, :], HG[0:rows, f % (LAG + 1), :], start=False, stop=(f == NF - 1)).then_inc(s.down_done, 1)
                                return
                            pe.wait_ge(s.hgl_done, f + 1)
                            nc.tensor.matmul(out, WDL[:, f, :], HGH[:, f % (LAG + 1), :], start=(f == 0), stop=False)
                            nc.tensor.matmul(out, WDH[:, f, :], HGL[:, f % (LAG + 1), :], start=False, stop=False)
                            nc.tensor.matmul(out, WDH[:, f, :], HGH[:, f % (LAG + 1), :], start=False, stop=False).then_inc(s.down_done, 1)

                        for f in range(NF):
                            hidden(f)
                            if f == 1 and not first:
                                turn_output(pe, s, spare)
                            if f >= LAG:
                                down(f - LAG)
                            if f == FT + 1 and not final:
                                pe.wait_ge(s.hg_done, FT)
                                pe.wait_ge(s.xhat_ready, 1)
                                transpose_input().then_inc(s.xt_done, 1)
                            if f == NF - 1 and not final:
                                pe.wait_ge(s.routed, 1)
                                transpose_routing().then_inc(s.ct_done, 1)
                            if first and f == 1:
                                output_product(s, spare)
                            if first and f == FT - 1:
                                pe.wait_ge(s.xh2_ready, 1)
                                for t in range(NT):
                                    last = nc.tensor.transpose(spare[:, t * P:(t + 1) * P], XH2[:, t, :], ident[:, :])
                                last.then_inc(s.xt2_done, 1)
                            if first and f == FT:
                                pe.wait_ge(s.xt2_ready, 1)
                                for t in range(NT):
                                    last = nc.tensor.matmul(spare[:, t * E:(t + 1) * E], XT2[:, t * P:(t + 1) * P], GW[:, :], start=True, stop=True)
                                last.then_inc(s.logits_done, 1)
                        for f in range(NF - LAG, NF):
                            down(f)

                    @block.scalar
                    def _(act):
                        if not first:
                            take_output(s, spare)
                        for f, (_, rows) in enumerate(FTILES):
                            act.wait_ge(s.g_done, f + 1)
                            if f >= 2:
                                act.wait_ge(s.tu_done, f - 1)
                            nc.scalar.activation(SG[0:rows, f % 2, :], G[f % 2][0:rows, :], ACT.Silu).then_inc(s.silu_done, 1)
                            if 1 <= f <= SPLIT:
                                act.wait_ge(s.hg_done, f)
                                if f > LAG + 1:
                                    act.wait_ge(s.down_done, f - LAG - 1)
                                nc.scalar.activation(HGH[:, (f - 1) % (LAG + 1), :], HG[:, (f - 1) % (LAG + 1), :], ACT.Copy).then_inc(s.hgh_done, 1)
                            if first and f == FT - 1:
                                act.wait_ge(s.xt2_done, 1)
                                nc.scalar.activation(XT2[:, :], spare[:, :], ACT.Copy).then_inc(s.xt2_ready, 1)
                            if first and f == FT:
                                act.wait_ge(s.logits_done, 1)
                                nc.scalar.activation(LG[:, LAST, :], spare[:, 0:NT * E].rearrange("p (t e) -> p t e", e=E), ACT.Copy).then_inc(s.logits_ready, 1)
                            if f == FT + 1 and not final:
                                take_coming(act, s, 1 - hf)
                        if not final:
                            take_routing(act, s, 1 - hf)
                        if first:
                            act.wait_ge(s.exp_in, 1)
                            nc.scalar.activation(LG[:, LAST, :], LG[:, LAST, :], ACT.Exp)

                    @block.gpsimd
                    def _(pool):
                        norm = norms(s)
                        if first:
                            nc.gpsimd.tensor_tensor(WDL[:, :, :], WD[:, 0:SPLIT, :], WDH[:, :, :].bitcast(F32), ALU.subtract)
                        for f in range(SPLIT):
                            pool.wait_ge(s.hgh_done, f + 1)
                            if f > LAG:
                                pool.wait_ge(s.down_done, f - LAG)
                            nc.gpsimd.tensor_tensor(HGL[:, f % (LAG + 1), :], HG[:, f % (LAG + 1), :], HGH[:, f % (LAG + 1), :].bitcast(F32), ALU.subtract).then_inc(s.hgl_done, 1)
                            if first:
                                if f == 0:
                                    norm.roots(pool, 1, [1])
                                elif f == 2:
                                    norm.roots(pool, 2, [0])
                                elif f == 4:
                                    add_normed(pool, s, NG)
                                elif f == 6:
                                    norm.roots(pool, 3, [0])
                            else:
                                if f == 2:
                                    norm.roots(pool, 1 if final else 2, [0] if final else [0, 1])
                                elif f == 4:
                                    add_normed(pool, s, g)

                    @block.vector
                    def _(v):
                        link, norm = Link(v, s.link), norms(s)

                        def unit(f):
                            rows = FTILES[f][1]
                            v.wait_ge(s.silu_done, f + 1)
                            v.wait_ge(s.u_done, f + 1)
                            if LAG < f < SPLIT + LAG + 1:
                                v.wait_ge(s.hgl_done, f - LAG)
                            if f >= FT:
                                ins = nc.vector.tensor_tensor(HG[0:rows, f % (LAG + 1), :], SG[0:rows, f % 2, :], U[f % 2][0:rows, :], ALU.mult)
                                ins.then_inc(s.tu_done, 1)
                                v.wait_ge(s.tu_done, f + 1)
                                v.sem_inc(s.hg_done, 1)
                                return
                            nc.vector.tensor_tensor(TU[:, f % 2, :], SG[:, f % 2, :], U[f % 2][:, :], ALU.mult).then_inc(s.tu_done, 1)
                            v.wait_ge(s.tu_done, f + 1)
                            nc.vector.tensor_tensor(HG[:, f % (LAG + 1), :], TU[:, f % 2, :], C[f % 2][:, :], ALU.mult).then_inc(s.hg_done, 1)

                        coming, attended = lambda t: group_tile(g + 1, t), lambda t: OSUM[:, t, :]
                        made = lambda t: spare[:, t * P:(t + 1) * P]
                        for f in range(NF):
                            unit(f)
                            if not final:
                                if f == (1 if first else 2):
                                    norm.statistics(link, 1, coming)
                                elif f == 6:
                                    norm.apply(v, 1, 1, coming, lambda t: XHAT[:, t, :]).then_inc(s.xhat_ready, 1)
                                elif 7 <= f < 7 + PARTS:
                                    route(link, f - 7, g + 1, s.routed)
                                elif f == NF - 1:
                                    coming_remainder(v, s, 1 - hf)
                            if not first:
                                if f == 1:
                                    v.wait_ge(s.y_turned, 1)
                                    norm.statistics(link, 0, made)
                                elif f == 5:
                                    norm.apply(v, 0, 1, made, attended).then_inc(s.normed, 1)
                            else:
                                if f == 2:
                                    add_residual(v, s, spare, (NG - 1) % 2)
                                    norm.statistics(link, 0, attended)
                                elif f == 4:
                                    norm.apply(v, 0, 2, attended, attended).then_inc(s.normed, 1)
                                elif f == 6:
                                    v.wait_ge(s.x_final, 1)
                                    norm.statistics(link, 0, lambda t: group_tile(NG - 1, t))
                                elif f == 8:
                                    norm.apply(v, 0, 3, lambda t: group_tile(NG - 1, t), lambda t: XH2[:, t, :]).then_inc(s.xh2_ready, 1)
                                elif f == FT + 1:
                                    v.wait_ge(s.logits_ready, 1)
                                    centre(link, LAST, s.exp_in)

            def take_output(s, bank):
                nc.scalar.activation(YS[:, :], bank[:, :], ACT.Copy).then_inc(s.y_out, 1)

            def turn_output(pe, s, bank):
                pe.wait_ge(s.y_out, 1)
                for t in range(NT):
                    last = nc.tensor.transpose(bank[:, t * P:(t + 1) * P], YS[:, t * P:(t + 1) * P], ident[:, :])
                last.then_inc(s.y_turned, 1)

            def add_normed(pool, s, g):
                pool.wait_ge(s.normed, 1)
                x = group_of(X, g - 1)
                nc.gpsimd.tensor_tensor(x, x, OSUM[:, :, :], ALU.add).then_inc(s.x_final, 1)

            moe_block(0, 0, first=True)
            with nc.Fori(0, NG // 2 - 1) as b:
                moe_block(b * 2 + 1, 1)
                moe_block(b * 2 + 2, 0)
            moe_block(NG - 1, 1, final=True)

            with nc.Block() as block:
                s = M[1]

                @block.scalar
                def _(act):
                    take_output(s, Y[1])

                @block.tensor
                def _(pe):
                    turn_output(pe, s, Y[1])

                @block.vector
                def _(v):
                    v.wait_ge(s.y_turned, 1)
                    norms(s)(v, Link(v, s.link), 1, lambda t: Y[1][:, t * P:(t + 1) * P], lambda t: OSUM[:, t, :]).then_inc(s.normed, 1)
                    v.wait_ge(s.normed, 1)
                    nc.vector.tensor_tensor(group_of(X, NG - 1), group_of(X, NG - 1), OSUM[:, :, :], ALU.add).then_inc(s.x_final, 1)

                @block.gpsimd
                def _(pool):
                    norms(s).roots(pool, 1, [0])

                @block.sync
                def _(sp):
                    store(sp, s, NG)
                    sp.wait_ge(stored, NG * 16)


_INS = ["L0_attn_x", "L0_attn_Wq", "L0_attn_Wk", "L0_attn_Wv", "L0_attn_Wa", "L0_attn_ba", "L0_attn_Wo", "L0_attn_gamma",
        "L0_attn_beta", "L0_ffn_gate_w", "L0_ffn_w_gate", "L0_ffn_w_up", "L0_ffn_w_down", "L0_ffn_sw_gate",
        "L0_ffn_sw_up", "L0_ffn_sw_down"]


def constants():
    import numpy as np

    n = np.arange(P)
    j, i = n[:, None], n[None, :]
    at_level = lambda s: (j // (2 * s) == i // (2 * s)) & (j // s % 2 == 0) & (i // s % 2 == 1)
    masks = np.stack([at_level(1), at_level(2), at_level(4), at_level(8)], axis=1)
    unit_expert = np.arange(EF).reshape(FT, P) // F
    return {
        "ident": np.eye(P, dtype=np.float32),
        "masks": masks.astype(np.uint32),
        "sel": (np.arange(2 * E)[:, None, None] % E == unit_expert[None]).astype(np.float32),
        "rank": np.broadcast_to(np.arange(E, 0, -1, dtype=np.float32), (P, E)).copy(),
    }


def kernel(**inputs):
    import numpy as _np
    import concourse.bacc as _bacc
    from concourse import mybir as _mybir
    from concourse.bass_utils import run_bass_kernel_spmd as _run

    nc = _bacc.Bacc("TRN2", target_bir_lowering=False, num_devices=1)
    arrays, args = {}, []
    given = {f"in_{n}": _np.ascontiguousarray(inputs[n]) for n in _INS}
    for name, a in {**given, **{f"const_{n}": a for n, a in constants().items()}}.items():
        arrays[name] = a
        args.append(nc.dram_tensor(name, a.shape, _mybir.dt.from_np(a.dtype), kind="ExternalInput").ap())
    out = nc.dram_tensor("out_0", (B, SEQ, D), F32, kind="ExternalOutput").ap()
    build(nc, *args, out)
    r = _run(nc, [arrays], core_ids=[0])
    return r.results[0]["out_0"]
```
